# Optimizing a Trainium2 kernel written in Bass

```python
import numpy as np
import jax
import jax.numpy as jnp

def _softmax(x, axis=-1):
    return jax.nn.softmax(x, axis=axis)

def _gelu(x):
    return jax.nn.gelu(x, approximate=True)

def _silu(x):
    return jax.nn.silu(x)

def _sigmoid(x):
    return jax.nn.sigmoid(x)

def _layernorm(x, axis=-1, eps=1e-05):
    m = jnp.mean(x, axis=axis, keepdims=True)
    v = jnp.var(x, axis=axis, keepdims=True)
    return (x - m) / jnp.sqrt(v + eps)

def _scatter_add(tgt, idx, src, axis=0):
    return tgt.at[idx].add(src)

def _segment_sum(src, seg, n):
    return jax.ops.segment_sum(src, seg, n)
kernel_name = 'mk_seq_preln_d1_jaxref_r8_b1db75'

def setup_inputs(seed: int=0):
    np.random.seed(seed)
    _w = jnp.asarray

    def _L0_attn_setup():
        import jax, jax.numpy as jnp
        import numpy as np
        import math
        D_MODEL = 128
        NUM_HEADS = 16
        HEAD = D_MODEL // NUM_HEADS
        EPS = 1e-05

        def _layernorm(x, w, b):
            mean = jnp.mean(x, axis=-1, keepdims=True)
            var = jnp.var(x, axis=-1, keepdims=True)
            return (x - mean) * w / jnp.sqrt(var + EPS) + b
        key = jax.random.key(seed)
        ks = jax.random.split(key, 5)
        x = jax.random.normal(ks[0], (2, 256, D_MODEL), dtype=jnp.float32)
        wq = jax.random.uniform(ks[1], (NUM_HEADS, D_MODEL, HEAD), dtype=jnp.float32) * 0.02
        wk = jax.random.uniform(ks[2], (NUM_HEADS, D_MODEL, HEAD), dtype=jnp.float32) * 0.02
        wv = jax.random.uniform(ks[3], (NUM_HEADS, D_MODEL, HEAD), dtype=jnp.float32) * 0.02
        wo = jax.random.uniform(ks[4], (D_MODEL, D_MODEL), dtype=jnp.float32) * 0.02
        ln_w = jnp.ones((D_MODEL,), dtype=jnp.float32)
        ln_b = jnp.zeros((D_MODEL,), dtype=jnp.float32)
        return {'x': x, 'ln_w': ln_w, 'ln_b': ln_b, 'wq': wq, 'wk': wk, 'wv': wv, 'wo': wo}
    _L0_attn_in = _L0_attn_setup()

    def _L0_ffn_setup():
        import jax, jax.numpy as jnp
        import numpy as np
        B, S, D, E, K = (2, 256, 128, 8, 2)
        H = 4 * D
        key = jax.random.key(seed)
        ks = jax.random.split(key, 6)
        x = jax.random.normal(ks[0], (B, S, D), dtype=jnp.float32)
        lim_g = np.sqrt(6.0 / (D + E)).astype(np.float32)
        W_gate = jax.random.uniform(ks[1], (D, E), minval=-lim_g, maxval=lim_g, dtype=jnp.float32)
        lim1 = np.sqrt(1.0 / D).astype(np.float32)
        lim2 = np.sqrt(1.0 / H).astype(np.float32)
        W1 = jax.random.uniform(ks[2], (E, D, H), minval=-lim1, maxval=lim1, dtype=jnp.float32)
        b1 = jax.random.uniform(ks[3], (E, H), minval=-lim1, maxval=lim1, dtype=jnp.float32)
        W2 = jax.random.uniform(ks[4], (E, H, D), minval=-lim2, maxval=lim2, dtype=jnp.float32)
        b2 = jax.random.uniform(ks[5], (E, D), minval=-lim2, maxval=lim2, dtype=jnp.float32)
        return {'x': x, 'W_gate': W_gate, 'W1': W1, 'b1': b1, 'W2': W2, 'b2': b2}
    _L0_ffn_in = _L0_ffn_setup()
    _d = {'L0_attn_x': _L0_attn_in['x'], 'L0_attn_ln_w': _L0_attn_in['ln_w'], 'L0_attn_ln_b': _L0_attn_in['ln_b'], 'L0_attn_wq': _L0_attn_in['wq'], 'L0_attn_wk': _L0_attn_in['wk'], 'L0_attn_wv': _L0_attn_in['wv'], 'L0_attn_wo': _L0_attn_in['wo'], 'L0_ffn_W_gate': _L0_ffn_in['W_gate'], 'L0_ffn_W1': _L0_ffn_in['W1'], 'L0_ffn_b1': _L0_ffn_in['b1'], 'L0_ffn_W2': _L0_ffn_in['W2'], 'L0_ffn_b2': _L0_ffn_in['b2']}
    _x0 = _d['L0_attn_x']
    _d['L0_attn_x'] = jax.random.normal(jax.random.fold_in(jax.random.key(seed), 1), (8, 512, 128), dtype=_x0.dtype)
    del _x0
    return _d

def reference(L0_attn_x, L0_attn_ln_w, L0_attn_ln_b, L0_attn_wq, L0_attn_wk, L0_attn_wv, L0_attn_wo, L0_ffn_W_gate, L0_ffn_W1, L0_ffn_b1, L0_ffn_W2, L0_ffn_b2):

    def _L0_attn_ref(x, ln_w, ln_b, wq, wk, wv, wo):
        import jax, jax.numpy as jnp
        import numpy as np
        import math
        D_MODEL = 128
        NUM_HEADS = 16
        HEAD = D_MODEL // NUM_HEADS
        EPS = 1e-05

        def _layernorm(x, w, b):
            mean = jnp.mean(x, axis=-1, keepdims=True)
            var = jnp.var(x, axis=-1, keepdims=True)
            return (x - mean) * w / jnp.sqrt(var + EPS) + b
        y = _layernorm(x, ln_w, ln_b)
        seq_len = y.shape[-2]
        q = jnp.einsum('bsd,hde->bhse', y, wq)
        k = jnp.einsum('bsd,hde->bhse', y, wk)
        v = jnp.einsum('bsd,hde->bhse', y, wv)
        scores = jnp.einsum('bhse,bhte->bhst', q, k) / math.sqrt(HEAD)
        causal = jnp.triu(jnp.full((seq_len, seq_len), -jnp.inf, dtype=scores.dtype), k=1)
        scores = scores + causal
        weights = jax.nn.softmax(scores, axis=-1)
        attn = jnp.einsum('bhst,bhte->bshe', weights, v)
        attn = attn.reshape(*attn.shape[:-2], -1)
        out = attn @ wo
        return out + x

    def _L0_ffn_ref(x, W_gate, W1, b1, W2, b2):
        import jax, jax.numpy as jnp
        import numpy as np
        B, S, D, E, K = (2, 256, 128, 8, 2)
        H = 4 * D
        gate = jnp.einsum('bsd,de->bse', x, W_gate)
        kth = jax.lax.top_k(gate, K)[0][..., -1:]
        mask = jax.nn.softmax(jnp.where(gate >= kth, gate, -jnp.inf), axis=-1)
        h = jax.nn.relu(jnp.einsum('bsd,edh->bseh', x, W1) + b1)
        y = jnp.einsum('bseh,ehd->bsed', h, W2) + b2
        return (y * mask[..., None]).mean(axis=-2)
    x = L0_attn_x
    x = x + _L0_attn_ref(_layernorm(x, axis=-1), L0_attn_ln_w, L0_attn_ln_b, L0_attn_wq, L0_attn_wk, L0_attn_wv, L0_attn_wo)
    x = x + _L0_ffn_ref(_layernorm(x, axis=-1), L0_ffn_W_gate, L0_ffn_W1, L0_ffn_b1, L0_ffn_W2, L0_ffn_b2)
    return x

_drawn_inputs = setup_inputs


def setup_inputs(seed=0):
    import zlib

    import numpy as np

    out = dict(_drawn_inputs(seed))
    spreads = {'L0_attn_ln_w': (1.0, 0.6), 'L0_attn_ln_b': (0.0, 0.8)}
    factors = {'L0_attn_wq': 8.0,
     'L0_attn_wk': 8.0,
     'L0_attn_wv': 8.0,
     'L0_attn_wo': 8.0,
     'L0_ffn_W_gate': 5.515,
     'L0_ffn_W1': 6.025,
     'L0_ffn_b1': 42.889,
     'L0_ffn_W2': 4.958,
     'L0_ffn_b2': 173.132}
    for name, (base, spread) in spreads.items():
        noise = np.random.default_rng([zlib.crc32(name.encode()), seed]).standard_normal(out[name].shape)
        drawn = base * np.exp(spread * noise) if base else spread * noise
        out[name] = jnp.asarray(drawn.astype(out[name].dtype))
    for name, factor in factors.items():
        out[name] = (out[name] * factor).astype(out[name].dtype)
    return out
```

```python
from contextlib import ExitStack

import concourse.bass as bass
from concourse import mybir

P = 128
F32 = mybir.dt.float32
F32R = mybir.dt.float32r
F16 = mybir.dt.float16
BF16 = mybir.dt.bfloat16
ALU = mybir.AluOpType
ACT = mybir.ActivationFunctionType
X = mybir.AxisListType.X
EPS = 1e-5
MASKED = -1e30
UNITS = 10


def schedule():
    steps, ffn = [], [0]

    def ffn_next(count):
        for _ in range(count):
            k = ffn[0]
            if k == 0:
                steps.append(("XE", 0))
            if k < 32:
                steps.append(("L1", k))
                if k % 4 == 0 and k < 28:
                    steps.append(("XE", k // 4 + 1))
            if 2 <= k < 34:
                steps.append(("L2", k - 2))
            ffn[0] += 1

    def head_tail(h):
        steps.append(("PM", h))
        if h >= 1:
            steps.append(("LO", h - 1))
        if h >= 3:
            steps.append(("PV", h - 3))
            if (h - 3) % 4 == 3:
                steps.append(("ON", (h - 3) // 4))

    def scores(g):
        for u in range(UNITS):
            if g < 4:
                steps.append(("MX", g, u))
            if g >= 1:
                steps.append(("ST", g - 1, u))
                if u % 5 == 4:
                    head_tail(4 * (g - 1) + 2 * (u // 5))
                if u in (1, 6) and 4 * (g - 1) + 2 * (u // 5) - 1 >= 0:
                    head_tail(4 * (g - 1) + 2 * (u // 5) - 1)
            if u % 3 == 2:
                ffn_next(1)
        if g < 4:
            steps.append(("NM", g))

    steps.append(("LN1",))
    steps.append(("ACC0",))
    ffn_next(4)
    steps.append(("YT",))
    ffn_next(2)
    for i in range(4):
        steps.append(("PJ", i))
    ffn_next(2)
    for g in range(4):
        steps.append(("KT", g))
        steps.append(("QT", g))
        if g >= 1:
            steps.append(("QM", g - 1))
        else:
            ffn_next(1)
        scores(g)
    steps.append(("QM", 3))
    scores(4)
    head_tail(15)
    steps.append(("LO", 15))
    ffn_next(2)
    for h in (13, 14, 15):
        steps.append(("PV", h))
    steps.append(("ON", 3))
    ffn_next(1)
    steps.append(("AT",))
    ffn_next(1)
    steps.append(("WO",))
    ffn_next(2)
    steps.append(("X2T",))
    ffn_next(1)
    steps.append(("GT",))
    ffn_next(2)
    steps.append(("MKT",))
    ffn_next(34 - ffn[0])
    steps.append(("OA",))
    steps.append(("OT",))
    return steps


STEPS = schedule()
FFN_STEPS = ("ACC0", "XE", "L1", "L2", "OA", "OT")
RING_STEPS = ("YT", "PJ", "KT", "QT", "MX", "QM", "AT", "WO", "X2T", "GT", "MKT")
RING_AT = {s: n for n, s in enumerate([s for s in STEPS if s[0] in RING_STEPS])}
RING = len(RING_AT)
L1_AT = {s: n for n, s in enumerate([s for s in STEPS if s[0] in ("XE", "L1")])}
L1_USES = len(L1_AT)
assert RING % 2 == 0 and L1_USES % 2 == 0 and sum(s[0] == "L2" for s in STEPS) == 32


def moe_block_kernel(nc, x, ln_w, ln_b, wqkv, wo, w_gate, w1, b1, w2, b2, out):
    B, S, D = x.shape
    E, _, H = w1.shape
    T = S // P
    HEADS, HD = 16, 8
    HG = 4
    R = 32
    C = H // P
    N1 = E * C
    BLK = 10
    SCALE = float(HD) ** -0.5
    VW = 32

    x_t = x.rearrange("b (t p) d -> b p t d", p=P)
    out_t = out.rearrange("b (t p) d -> b p t d", p=P)
    w1_t = w1.rearrange("e d h -> d e h")
    w2_t = w2.rearrange("e (c p) d -> p e c d", p=P)

    with ExitStack() as ctx:
        def sb(name, shape, dt=F32):
            return ctx.enter_context(nc.sbuf_tensor(name, shape, dt))

        def sem(name):
            return ctx.enter_context(nc.semaphore(name))

        ring = ctx.enter_context(nc.psum_tensor("ring", [P, 2, 512], F32))
        st_ps = ctx.enter_context(nc.psum_tensor("st_ps", [P, 2, 512], F32))
        l1_ps = ctx.enter_context(nc.psum_tensor("l1_ps", [P, 2, 512], F32))
        acc_ps = ctx.enter_context(nc.psum_tensor("acc_ps", [P, 512], F32))
        pv_ps = ctx.enter_context(nc.psum_tensor("pv_ps", [P, 512], F32))

        ident = sb("ident", [P, P])
        ident_b = sb("ident_b", [P, P], BF16)
        causal = sb("causal", [P, P], BF16)
        pick = sb("pick", [P, E, P], F32R)
        half_neg = sb("half_neg", [P, T])
        eps = sb("eps", [P, T])
        lnw = sb("lnw", [P, 1])
        lnb = sb("lnb", [P, 1])
        wqkv_s = sb("wqkv_s", [P, 3 * P])
        wo_s = sb("wo_s", [P, D])
        wg_s = sb("wg_s", [P, E])
        b1_s = sb("b1_s", [E, H])
        b2_x = sb("b2_x", [P, D], F32R)
        w1_hi = sb("w1_hi", [P, E, H], F32R)
        w1_lo = sb("w1_lo", [P, E, H], F32R)
        w2_hi = sb("w2_hi", [P, N1, D], F32R)
        w2_lo = sb("w2_lo", [P, N1, D], F32R)
        xb = sb("xb", [P, T, D])
        stats = sb("stats", [P, T, 6])
        mv = sb("mv", [P, T, 2])
        rs = sb("rs", [P, 6, T])
        yn = sb("yn", [P, T, D])
        xn = sb("xn", [P, T, D])
        xr = xn
        y_t = sb("y_t", [P, S])
        qk = sb("qk", [P, T, 2, HEADS, R])
        vr = sb("vr", [P, T, HEADS, HD])
        v_op = sb("v_op", [P, T, HEADS, VW], BF16)
        kz = sb("kz", [P, 2, HG, S], F32R)
        q1 = sb("q1", [P, 2, S], F32R)
        q2 = sb("q2", [P, 2, S], F32R)
        bmax = sb("bmax", [P, HEADS, BLK])
        nmax = sb("nmax", [P, T, HG])
        p32 = sb("p32", [P, 4, BLK * P])
        p_hi = sb("p_hi", [P, 4, BLK * P], F16)
        p_lo = sb("p_lo", [P, 4, BLK * P], F16)
        osum = sb("osum", [P, T * HG, HD])
        rden = sb("rden", [P, T * HG])
        attn = sb("attn", [P, T, HEADS, HD])
        a_t = y_t
        x1 = sb("x1", [P, T, D])
        xn2 = yn
        x2_t = sb("x2_t", [P, S])
        gate = sb("gate", [P, T, E])
        top = sb("top", [P, T, 8])
        gsel = sb("gsel", [P, T, E])
        gexp = sb("gexp", [P, T, E])
        gsum = sb("gsum", [P, T])
        m_tok = sb("m_tok", [P, T, P])
        m_t = sb("m_t", [P, S], F32R)
        xe = sb("xe", [P, 2, S])
        xe_hi = sb("xe_hi", [P, 2, S], F32R)
        xe_lo = sb("xe_lo", [P, 2, S], F32R)
        stage = p32[:, :, 0:H]
        pick_f = p32[:, :, H:H + 2 * P].rearrange("p a (b k) -> p a b k", b=2)
        w1c = xe
        mean_w = attn[:, 0, :, :].rearrange("p h e -> p (h e)")
        b2_f = osum[:, :, :].rearrange("p n e -> p (n e)")
        h_hi = sb("h_hi", [P, 3, S], F32R)
        h_lo = sb("h_lo", [P, 3, S], F32R)
        acc_s = sb("acc_s", [P, S])
        ob = sb("ob", [P, T, D])

        consts_loaded = sem("consts_loaded")
        stage_loaded = [sem(f"stage_loaded{k}") for k in range(4)]
        x_loaded = sem("x_loaded")
        out_stored = sem("out_stored")
        waited_apart = sem("waited_apart")
        tables_set = sem("tables_set")
        consts_built = sem("consts_built")
        b1_scaled = sem("b1_scaled")
        w1_mean = sem("w1_mean")
        w1_centred = sem("w1_centred")
        w_hi_ready = sem("w_hi_ready")
        w_lo_ready = sem("w_lo_ready")
        b2_hi_ready = sem("b2_hi_ready")
        pick_ready = sem("pick_ready")
        stats_ready = sem("stats_ready")
        rs_step = sem("rs_step")
        rstd_ready = sem("rstd_ready")
        xn_ready = sem("xn_ready")
        xr_ready = sem("xr_ready")
        ring_filled = sem("ring_filled")
        y_t_ready = sem("y_t_ready")
        qk_hi_ready = sem("qk_hi_ready")
        qk_lo_ready = sem("qk_lo_ready")
        v1_ready = sem("v1_ready")
        v_rest_ready = sem("v_rest_ready")
        v2_ready = sem("v2_ready")
        v3_ready = sem("v3_ready")
        kz_ready = sem("kz_ready")
        q1_ready = sem("q1_ready")
        q2_ready = sem("q2_ready")
        bmax_ready = sem("bmax_ready")
        nmax_ready = sem("nmax_ready")
        m_cleared = sem("m_cleared")
        m_hi_ready = sem("m_hi_ready")
        m_ready = sem("m_ready")
        st_filled = sem("st_filled")
        exp_ready = sem("exp_ready")
        p_masked = sem("p_masked")
        p_hi_ready = sem("p_hi_ready")
        p_lo_ready = sem("p_lo_ready")
        pv_done = sem("pv_done")
        osum_ready = sem("osum_ready")
        pv_read = sem("pv_read")
        attn_ready = sem("attn_ready")
        a_t_ready = sem("a_t_ready")
        x1_ready = sem("x1_ready")
        xn2_ready = sem("xn2_ready")
        x2_t_ready = sem("x2_t_ready")
        gate_step = sem("gate_step")
        gexp_ready = sem("gexp_ready")
        m_tok_ready = sem("m_tok_ready")
        m_t_ready = sem("m_t_ready")
        xe_ready = sem("xe_ready")
        xe_hi_ready = sem("xe_hi_ready")
        xe_lo_ready = sem("xe_lo_ready")
        acc_begun = sem("acc_begun")
        l1_filled = sem("l1_filled")
        h_hi_ready = sem("h_hi_ready")
        h_lo_ready = sem("h_lo_ready")
        l2_done = sem("l2_done")
        acc_saved = sem("acc_saved")
        ot_filled = sem("ot_filled")
        ob_ready = sem("ob_ready")

        def since(eng, signal, value):
            if not (isinstance(value, int) and value <= 0):
                eng.wait_ge(signal, value)

        def read_by(step, b):
            k, g = step[0], (step[1] if len(step) > 1 else 0)
            return {
                "YT": lambda: (y_t_ready, b + 1),
                "PJ": lambda: (qk_lo_ready, T * b + g + 1),
                "KT": lambda: (kz_ready, HEADS * b + HG * g + HG),
                "QT": lambda: (q1_ready, HG * b + g + 1),
                "QM": lambda: (q2_ready, HG * b + g + 1),
                "MX": lambda: (bmax_ready, 40 * b + UNITS * g + step[2] + 1),
                "AT": lambda: (a_t_ready, b + 1),
                "WO": lambda: (x1_ready, b + 1),
                "X2T": lambda: (x2_t_ready, b + 1),
                "GT": lambda: (gate_step, 8 * b + 1),
                "MKT": lambda: (m_t_ready, b + 1),
                "XE": lambda: (xe_ready, E * b + g + 1),
                "L1": lambda: (h_lo_ready, N1 * b + g + 1),
            }[k]()

        def apart(eng):
            eng.sem_inc(waited_apart, 1)

        def bank_free(eng, at, step, b):
            users = list(at)
            n = at[step] - 2
            if n >= 0:
                eng.wait_ge(*read_by(users[n], b))
            else:
                signal, value = read_by(users[-1], b - 1)
                since(eng, signal, value)

        def ring_full(eng, step, b):
            eng.wait_ge(ring_filled, RING * b + RING_AT[step] + 1)

        def unit(g, u):
            pair, v = u // 5, u % 5
            head = 2 * pair + (1 if v in (2, 3) else 0)
            return pair, v, head

        def run(steps, one, b, f):
            for s in steps:
                one(s, b, f)

        first = [s for s in STEPS if s[0] not in FFN_STEPS]
        last = [s for s in STEPS if s[0] in FFN_STEPS]

        block = ctx.enter_context(nc.Block())

        @block.sync
        def _(sp):
            sp.dma_start(xb[:, :, :], x_t[0]).then_inc(x_loaded, 16)
            for dst, src in ((lnw[:, :], ln_w.rearrange("(d a) -> d a", a=1)), (lnb[:, :], ln_b.rearrange("(d a) -> d a", a=1)),
                             (wqkv_s[:, :], wqkv), (wo_s[:, :], wo), (wg_s[:, :], w_gate),
                             (b1_s[:, :], b1)):
                sp.dma_start(dst, src).then_inc(consts_loaded, 16)
            sp.wait_ge(tables_set, 1)
            for k in range(3):
                sp.dma_start(b2_f[32 * k:32 * k + E, :], b2).then_inc(consts_loaded, 16)
            for n in range(2 * E):
                e = n % E
                if n >= 4:
                    sp.wait_ge(w_lo_ready, n - 3)
                src = w1_t[:, e, :] if n < E else w2_t[:, e, :, :]
                dst = stage[:, n % 4, :] if n < E else stage[:, n % 4, :].rearrange("p (c d) -> p c d", c=C)
                sp.dma_start(dst, src).then_inc(stage_loaded[n % 4], 16)

            def load(b, src):
                sp.wait_ge(xr_ready, b + 1)
                sp.dma_start(xb[:, :, :], src).then_inc(x_loaded, 16)

            def store(f, dst):
                sp.wait_ge(ob_ready, f + 1)
                sp.dma_start(dst, ob[:, :, :]).then_inc(out_stored, 16)

            load(0, x_t[1])
            with sp.Fori(1, B - 1) as b:
                load(b, x_t[bass.ds(b + 1, 1)].rearrange("a p t d -> p (a t) d"))
                store(b - 1, out_t[bass.ds(b - 1, 1)].rearrange("a p t d -> p (a t) d"))
            store(B - 2, out_t[B - 2])
            store(B - 1, out_t[B - 1])
            sp.wait_ge(out_stored, 16 * B)

        @block.gpsimd
        def _(pool):
            g = nc.gpsimd
            g.memset(b2_f[:, :], 0.0).then_inc(tables_set, 1)
            g.memset(ident[:, :], 0.0)
            g.memset(causal[:, :], 0.0)
            g.memset(pick_f, 0.0)
            g.memset(mean_w[:, :], 1.0 / D)
            g.memset(half_neg[:, :], -0.5)
            g.memset(eps[:, :], EPS)
            g.memset(qk[:, :, :, :, :], 0.0)
            g.memset(v_op[:, :, :, 3 * HD:VW], 1.0)
            g.memset(m_tok[:, :, :], 0.0)
            g.memset(kz[:, :, :, :].bitcast(F32), 0.0).then_inc(tables_set, 1)
            pool.wait_ge(tables_set, 2)
            g.affine_select(out=ident[:, :], in_=ident[:, :], compare_op=ALU.not_equal, fill=1.0, base=0,
                            pattern=[[-1, P]], channel_multiplier=1)
            g.affine_select(out=causal[:, :], in_=causal[:, :], compare_op=ALU.is_ge, fill=MASKED, base=0,
                            pattern=[[-1, P]], channel_multiplier=1)
            g.memset(qk[:, :, 1, :, 3 * HD:3 * HD + 2], 1.0)
            g.affine_select(out=pick_f, in_=pick_f, compare_op=ALU.not_equal, fill=1.0, base=0,
                            pattern=[[-2, 4], [-1, 2], [0, P]], channel_multiplier=1).then_inc(tables_set, 1)
            pool.wait_ge(tables_set, 3)
            g.tensor_copy(ident_b[:, :], ident[:, :])
            g.affine_select(out=pick_f, in_=pick_f, compare_op=ALU.not_equal, fill=1.0, base=-32,
                            pattern=[[-2, 4], [-1, 2], [0, P]], channel_multiplier=1).then_inc(consts_built, 1)

            def weights():
                for n in range(2 * E):
                    e = n % E
                    pool.wait_ge(w_hi_ready, n + 1)
                    if n < E:
                        g.tensor_tensor(w1_lo[:, e, :], w1c[:, n % 2, :], w1_hi[:, e, :].bitcast(F32), ALU.subtract).then_inc(w_lo_ready, 1)
                    else:
                        g.tensor_tensor(w2_lo[:, C * e:C * e + C, :], stage[:, n % 4, :].rearrange("p (c d) -> p c d", c=C),
                                        w2_hi[:, C * e:C * e + C, :].bitcast(F32), ALU.subtract).then_inc(w_lo_ready, 1)

            def power(dst, src, n):
                pool.wait_ge(rs_step, n)
                return g.tensor_tensor(dst, src, half_neg[:, :], ALU.pow)

            def one(s, b, f):
                k = s[0]
                if k == "LN1":
                    pool.wait_ge(stats_ready, 4 * b + 2)
                    z = 8 * b
                    g.tensor_tensor(rs[:, 0, :], mv[:, :, 1], eps[:, :], ALU.add).then_inc(rs_step, 1)
                    power(rs[:, 1, :], rs[:, 0, :], z + 1).then_inc(rs_step, 1)
                    pool.wait_ge(rs_step, z + 2)
                    g.tensor_tensor(rs[:, 2, :], rs[:, 1, :], mv[:, :, 1], ALU.mult).then_inc(rs_step, 1)
                    pool.wait_ge(rs_step, z + 3)
                    g.tensor_tensor(rs[:, 3, :], rs[:, 2, :], rs[:, 1, :], ALU.mult).then_inc(rs_step, 1)
                    pool.wait_ge(rs_step, z + 4)
                    g.tensor_tensor(rs[:, 4, :], rs[:, 3, :], eps[:, :], ALU.add).then_inc(rs_step, 1)
                    power(rs[:, 5, :], rs[:, 4, :], z + 5).then_inc(rs_step, 1)
                    pool.wait_ge(rs_step, z + 6)
                    g.tensor_tensor(rs[:, 0, :], rs[:, 5, :], rs[:, 1, :], ALU.mult).then_inc(rstd_ready, 1)
                    pool.wait_ge(xn_ready, b + 1)
                    g.tensor_tensor(xr[:, :, :], xb[:, :, :], xn[:, :, :], ALU.add).then_inc(xr_ready, 1)
                    since(pool, q2_ready, HG * b)
                    apart(pool)
                    g.memset(qk[:, :, 0, :, 3 * HD:3 * HD + 2], 0.0).then_inc(m_cleared, 1)
                elif k == "PJ":
                    if s[1] == T - 1:
                        pool.wait_ge(v2_ready, b + 1)
                        g.tensor_tensor(v_op[:, :, :, 2 * HD:3 * HD], vr[:, :, :, :], v_op[:, :, :, HD:2 * HD],
                                        ALU.subtract).then_inc(v3_ready, 1)
                elif k == "PM":
                    h = s[1]
                    pool.wait_ge(exp_ready, 40 * b + 10 * (h // 4) + 5 * (h % 4 // 2) + 5)
                    apart(pool)
                    v = p32[:, h % 4, 0:T * P].rearrange("p (t s) -> p t s", t=T)
                    g.affine_select(out=v, in_=v, compare_op=ALU.is_ge, fill=0.0, base=0,
                                    pattern=[[0, T], [1, P]], channel_multiplier=-1).then_inc(p_masked, 1)
                elif k == "LO":
                    h = s[1]
                    pool.wait_ge(p_hi_ready, HEADS * b + h + 1)
                    since(pool, pv_done, HEADS * b + h - 3)
                    g.tensor_tensor(p_lo[:, h % 4, :], p32[:, h % 4, :], p_hi[:, h % 4, :], ALU.subtract).then_inc(p_lo_ready, 1)
                elif k == "X2T":
                    pool.wait_ge(stats_ready, 4 * b + 4)
                    g.tensor_tensor(rs[:, 0, :], mv[:, :, 1], eps[:, :], ALU.add).then_inc(rs_step, 1)
                    pool.wait_ge(rs_step, 8 * b + 7)
                    g.tensor_tensor(rs[:, 1, :], rs[:, 0, :], half_neg[:, :], ALU.pow).then_inc(rs_step, 1)
                elif k == "XE":
                    e = s[1]
                    pool.wait_ge(xe_hi_ready, E * f + e + 1)
                    g.tensor_tensor(xe_lo[:, e % 2, :], xe[:, e % 2, :], xe_hi[:, e % 2, :].bitcast(F32), ALU.subtract).then_inc(xe_lo_ready, 1)

            run(first[:6], one, 0, None)
            weights()
            run(first[6:], one, 0, None)
            run(STEPS, one, 1, 0)
            with pool.Fori(2, B) as b:
                run(STEPS, one, b, b - 1)
            run(last, one, None, B - 1)

        @block.scalar
        def _(act):
            a = nc.scalar
            copy = ACT.Copy

            def weights():
                act.wait_ge(consts_built, 1)
                a.activation(pick[:, :, :].rearrange("p (a b) k -> p a b k", b=2), pick_f, copy).then_inc(pick_ready, 1)
                act.wait_ge(consts_loaded, 16 * 9)
                a.activation(b1_s[:, :], b1_s[:, :], copy, scale=-1.0 / D).then_inc(b1_scaled, 1)
                a.activation(b2_x[:, :], b2_f[:, :], copy).then_inc(b2_hi_ready, 1)
                for n in range(2 * E):
                    e = n % E
                    if n < E:
                        act.wait_ge(w1_centred, n + 1)
                        a.activation(w1_hi[:, e, :], w1c[:, n % 2, :], copy).then_inc(w_hi_ready, 1)
                    else:
                        act.wait_ge(stage_loaded[n % 4], 16 * (n // 4 + 1))
                        a.activation(w2_hi[:, C * e:C * e + C, :], stage[:, n % 4, :].rearrange("p (c d) -> p c d", c=C),
                                     copy).then_inc(w_hi_ready, 1)

            def one(s, b, f):
                k = s[0]
                bank = RING_AT.get(s, 0) % 2
                if k == "YT":
                    ring_full(act, s, b)
                    if isinstance(b, int):
                        act.wait_ge(consts_loaded, 16 * 9)
                    a.activation(y_t[:, :], ring[:, bank, :], ACT.Identity, bias=lnb[:, 0:1], scale=lnw[:, 0:1]).then_inc(y_t_ready, 1)
                elif k == "PJ":
                    i = s[1]
                    ring_full(act, s, b)
                    since(act, pv_done, HEADS * b)
                    a.activation(v_op[:, i, :, 0:HD], ring[:, bank, 2 * P:3 * P].rearrange("p (h e) -> p h e", e=HD), copy).then_inc(v1_ready, 1)
                    v = qk[:, i, :, :, 0:HD].rearrange("p k h e -> p (k h) e")
                    a.activation(v.bitcast(F32R), ring[:, bank, 0:2 * P].rearrange("p (h e) -> p h e", e=HD),
                                 copy).then_inc(qk_hi_ready, 1)
                elif k == "KT":
                    g = s[1]
                    ring_full(act, s, b)
                    for hh in range(HG):
                        rows = slice(R * hh, R * hh + R)
                        a.activation(kz[rows, g % 2, hh, :], ring[rows, bank, :], copy).then_inc(kz_ready, 1)
                elif k == "QT":
                    g = s[1]
                    ring_full(act, s, b)
                    a.activation(q1[:, g % 2, :], ring[:, bank, :], copy).then_inc(q1_ready, 1)
                elif k == "QM":
                    g = s[1]
                    ring_full(act, s, b)
                    a.activation(q2[:, g % 2, :], ring[:, bank, :], copy).then_inc(q2_ready, 1)
                elif k == "ST":
                    g, u = s[1], s[2]
                    pair, v, head = unit(g, u)
                    act.wait_ge(st_filled, 40 * b + 10 * g + u + 1)
                    if isinstance(b, int):
                        act.wait_ge(w_lo_ready, 2 * E)
                    since(act, p_lo_ready, HEADS * b + 4 * g + 2 * pair - 2)
                    slot = (4 * g + head) % 4
                    if v in (0, 2):
                        dst, src = p32[:, slot, 0:512], st_ps[:, (10 * g + u) % 2, :]
                    elif v in (1, 3):
                        dst, src = p32[:, slot, 512:1024], st_ps[:, (10 * g + u) % 2, :]
                    else:
                        dst = p32[:, 2 * pair:2 * pair + 2, 1024:1280]
                        src = st_ps[:, (10 * g + u) % 2, :].rearrange("p (h s) -> p h s", h=2)
                    a.activation(dst, src, ACT.Exp, scale=SCALE).then_inc(exp_ready, 1)
                elif k == "AT":
                    ring_full(act, s, b)
                    a.activation(a_t[:, :], ring[:, bank, :], copy).then_inc(a_t_ready, 1)
                elif k == "X2T":
                    ring_full(act, s, b)
                    since(act, xe_ready, E * b)
                    a.activation(x2_t[:, :], ring[:, bank, :], copy).then_inc(x2_t_ready, 1)
                elif k == "GT":
                    act.wait_ge(gate_step, 8 * b + 3)
                    a.activation(gexp[:, :, :], gate[:, :, :], ACT.Exp).then_inc(gexp_ready, 1)
                elif k == "MKT":
                    ring_full(act, s, b)
                    since(act, xe_ready, E * b)
                    a.activation(m_t[:, :], ring[:, bank, :], copy).then_inc(m_t_ready, 1)
                elif k == "XE":
                    e = s[1]
                    act.wait_ge(xe_ready, E * f + e + 1)
                    a.activation(xe_hi[:, e % 2, :], xe[:, e % 2, :], copy).then_inc(xe_hi_ready, 1)
                elif k == "L1":
                    n = s[1]
                    act.wait_ge(l1_filled, L1_USES * f + L1_AT[s] + 1)
                    since(act, l2_done, N1 * f + max(n - 2, 0))
                    a.activation(h_hi[:, n % 3, :], l1_ps[:, L1_AT[s] % 2, :], ACT.Relu).then_inc(h_hi_ready, 1)
                elif k == "OA":
                    act.wait_ge(l2_done, N1 * f + N1)
                    since(act, ot_filled, f)
                    a.activation(acc_s[:, :], acc_ps[:, :], copy).then_inc(acc_saved, 1)

            run(first[:6], one, 0, None)
            weights()
            run(first[6:], one, 0, None)
            run(STEPS, one, 1, 0)
            with act.Fori(2, B) as b:
                run(STEPS, one, b, b - 1)
            run(last, one, None, B - 1)

        @block.vector
        def _(dve):
            v = nc.vector

            def norm_stats(src, z):
                for i in range(T):
                    last = v.bn_stats(stats[:, i, :], src[:, i, :])
                last.then_inc(stats_ready, 1)
                dve.wait_ge(stats_ready, z + 1)
                apart(dve)
                for i in range(T):
                    last = v.bn_aggr(mv[:, i, :], stats[:, i, :])
                last.then_inc(stats_ready, 1)

            def weights():
                dve.wait_ge(b2_hi_ready, 1)
                v.tensor_tensor(b2_x[64:64 + R, :], b2_f[64:64 + R, :], b2_x[64:64 + R, :].bitcast(F32), ALU.subtract).then_inc(b2_hi_ready, 1)
                for e in range(E):
                    dve.wait_ge(w1_mean, e + 1)
                    if e >= 2:
                        dve.wait_ge(w_lo_ready, e - 1)
                    v.tensor_tensor(w1c[:, e % 2, :], stage[:, e % 4, :], l1_ps[:, e % 2, :], ALU.subtract).then_inc(w1_centred, 1)

            def one(s, b, f):
                k = s[0]
                bank = RING_AT.get(s, 0) % 2
                if k == "LN1":
                    dve.wait_ge(x_loaded, 16 * b + 16)
                    since(dve, xn2_ready, b)
                    norm_stats(xb, 4 * b)
                    dve.wait_ge(rstd_ready, b + 1)
                    for i in range(T):
                        v.tensor_scalar(yn[:, i, :], xb[:, i, :], mv[:, i, 0:1], rs[:, 0, i:i + 1], ALU.subtract, ALU.mult)
                    since(dve, x1_ready, b)
                    for i in range(T):
                        last = v.tensor_scalar(xn[:, i, :], xb[:, i, :], mv[:, i, 0:1], rs[:, 1, i:i + 1], ALU.subtract, ALU.mult)
                    last.then_inc(xn_ready, 1)
                elif k == "PJ":
                    i = s[1]
                    dve.wait_ge(qk_hi_ready, T * b + i + 1)
                    v.tensor_tensor(vr[:, i, :, :], ring[:, bank, 2 * P:3 * P].rearrange("p (h e) -> p h e", e=HD),
                                    v_op[:, i, :, 0:HD], ALU.subtract).then_inc(v_rest_ready, 1)
                    v.tensor_copy(qk[:, i, 1, :, HD:2 * HD], qk[:, i, 1, :, 0:HD])
                    v.tensor_copy(qk[:, i, 0, :, 2 * HD:3 * HD], qk[:, i, 0, :, 0:HD])
                    v.tensor_tensor(qk[:, i, 0, :, HD:2 * HD], ring[:, bank, 0:P].rearrange("p (h e) -> p h e", e=HD),
                                    qk[:, i, 0, :, 0:HD], ALU.subtract)
                    v.tensor_tensor(qk[:, i, 1, :, 2 * HD:3 * HD], ring[:, bank, P:2 * P].rearrange("p (h e) -> p h e", e=HD),
                                    qk[:, i, 1, :, 0:HD], ALU.subtract).then_inc(qk_lo_ready, 1)
                    if i == T - 1:
                        dve.wait_ge(v_rest_ready, T * b + T)
                        v.tensor_copy(v_op[:, :, :, HD:2 * HD], vr[:, :, :, :]).then_inc(v2_ready, 1)
                elif k == "MX":
                    g, u = s[1], s[2]
                    pair, w, head = unit(g, u)
                    h = HG * g + head
                    ring_full(dve, s, b)
                    blocks = ring[:, bank, :].rearrange("p (k s) -> p k s", k=4)
                    if w in (0, 2):
                        dst = bmax[:, h, 0:4]
                    elif w in (1, 3):
                        dst = bmax[:, h, 4:8]
                    else:
                        dst = bmax[:, HG * g + 2 * pair:HG * g + 2 * pair + 2, 8:10]
                        blocks = ring[:, bank, :].rearrange("p (h k s) -> p h k s", h=2, k=2)
                    v.tensor_reduce(dst, blocks, X, ALU.max).then_inc(bmax_ready, 1)
                elif k == "NM":
                    g = s[1]
                    dve.wait_ge(bmax_ready, 40 * b + UNITS * g + UNITS)
                    dve.wait_ge(m_cleared, b + 1)
                    hs = slice(HG * g, HG * g + HG)
                    for i, (lo, hi) in enumerate(((7, 8), (8, 10), (4, 7), (0, 4))):
                        last = v.tensor_reduce(nmax[:, i, :], bmax[:, hs, lo:hi], X, ALU.max, negate=True)
                    last.then_inc(nmax_ready, 1)
                    dve.wait_ge(nmax_ready, HG * b + g + 1)
                    v.tensor_copy(qk[:, :, 0, hs, 3 * HD].bitcast(F32R), nmax[:, :, :]).then_inc(m_hi_ready, 1)
                    dve.wait_ge(m_hi_ready, HG * b + g + 1)
                    v.tensor_tensor(qk[:, :, 0, hs, 3 * HD + 1], nmax[:, :, :], qk[:, :, 0, hs, 3 * HD],
                                    ALU.subtract).then_inc(m_ready, 1)
                elif k == "PM":
                    h = s[1]
                    dve.wait_ge(p_masked, HEADS * b + h + 1)
                    since(dve, pv_done, HEADS * b + h - 3)
                    v.tensor_copy(p_hi[:, h % 4, :], p32[:, h % 4, :]).then_inc(p_hi_ready, 1)
                elif k == "ON":
                    g = s[1]
                    dve.wait_ge(pv_done, HEADS * b + HG * g + HG)
                    o = pv_ps[:, :].rearrange("p (n c) -> p n c", c=VW)
                    v.tensor_reduce(osum[:, :, :], o[:, :, 0:3 * HD].rearrange("p n (k e) -> p n e k", k=3), X, ALU.add)
                    v.reciprocal(rden[:, :], o[:, :, 3 * HD]).then_inc(pv_read, 1)
                    dve.wait_ge(pv_read, HG * b + g + 1)
                    for i in range(T):
                        r = rden[:, HG * i:HG * i + HG].rearrange("p (h a) -> p h a", a=1).broadcast_to([P, HG, HD])
                        last = v.tensor_tensor(attn[:, i, HG * g:HG * g + HG, :], osum[:, HG * i:HG * i + HG, :], r, ALU.mult)
                    last.then_inc(attn_ready, 1)
                    dve.wait_ge(attn_ready, HG * b + g + 1)
                elif k == "WO":
                    ring_full(dve, s, b)
                    dve.wait_ge(xr_ready, b + 1)
                    since(dve, acc_begun, b)
                    v.tensor_tensor(x1[:, :, :], ring[:, bank, :].rearrange("p (t d) -> p t d", t=T), xr[:, :, :],
                                    ALU.add).then_inc(x1_ready, 1)
                    dve.wait_ge(x1_ready, b + 1)
                    norm_stats(x1, 4 * b + 2)
                    dve.wait_ge(rs_step, 8 * b + 8)
                    for i in range(T):
                        last = v.tensor_scalar(xn2[:, i, :], x1[:, i, :], mv[:, i, 0:1], rs[:, 1, i:i + 1], ALU.subtract, ALU.mult)
                    last.then_inc(xn2_ready, 1)
                elif k == "GT":
                    z = 8 * b
                    ring_full(dve, s, b)
                    v.tensor_copy(gate[:, :, :], ring[:, bank, 0:T * E].rearrange("p (t e) -> p t e", t=T)).then_inc(gate_step, 1)
                    dve.wait_ge(gate_step, z + 1)
                    apart(dve)
                    for i in range(T):
                        last = v.max(top[:, i, :], gate[:, i, :])
                    last.then_inc(gate_step, 1)
                    dve.wait_ge(gate_step, z + 2)
                    v.tensor_tensor(gsel[:, :, :], gate[:, :, :], top[:, :, 1:2].broadcast_to([P, T, E]), ALU.is_ge)
                    v.tensor_tensor(gate[:, :, :], gate[:, :, :], top[:, :, 0:1].broadcast_to([P, T, E]), ALU.subtract).then_inc(gate_step, 1)
                    dve.wait_ge(gexp_ready, b + 1)
                    v.tensor_tensor(gsel[:, :, :], gexp[:, :, :], gsel[:, :, :], ALU.mult).then_inc(gate_step, 1)
                    dve.wait_ge(gate_step, z + 4)
                    v.tensor_reduce(gsum[:, :], gsel[:, :, :], X, ALU.add).then_inc(gate_step, 1)
                    dve.wait_ge(gate_step, z + 5)
                    v.reciprocal(gsum[:, :], gsum[:, :]).then_inc(gate_step, 1)
                    dve.wait_ge(gate_step, z + 6)
                    v.tensor_tensor(gate[:, :, :], gsel[:, :, :], gsum[:, :].rearrange("p (t a) -> p t a", a=1).broadcast_to([P, T, E]),
                                    ALU.mult).then_inc(gate_step, 1)
                    dve.wait_ge(gate_step, z + 7)
                    v.tensor_scalar(m_tok[:, :, 0:E].bitcast(F32R), gate[:, :, :], 1.0 / E, None, ALU.mult)
                    v.tensor_scalar(m_tok[:, :, 64:64 + E].bitcast(F32R), gate[:, :, :], 1.0 / E, None, ALU.mult).then_inc(gate_step, 1)
                    dve.wait_ge(gate_step, z + 8)
                    v.scalar_tensor_tensor(out=m_tok[:, :, 32:32 + E], in0=gate[:, :, :], scalar=1.0 / E, in1=m_tok[:, :, 0:E],
                                           op0=ALU.mult, op1=ALU.subtract).then_inc(m_tok_ready, 1)
                elif k == "XE":
                    e = s[1]
                    dve.wait_ge(l1_filled, L1_USES * f + L1_AT[s] + 1)
                    dve.wait_ge(x2_t_ready, f + 1)
                    since(dve, xe_lo_ready, E * f + max(e - 1, 0))
                    v.scalar_tensor_tensor(out=xe[:, e % 2, :], in0=x2_t[:, :], scalar=1.0, in1=l1_ps[:, L1_AT[s] % 2, :],
                                           op0=ALU.add, op1=ALU.mult).then_inc(xe_ready, 1)
                elif k == "L1":
                    n = s[1]
                    dve.wait_ge(h_hi_ready, N1 * f + n + 1)
                    since(dve, l2_done, N1 * f + max(n - 2, 0))
                    v.scalar_tensor_tensor(out=h_lo[:, n % 3, :], in0=l1_ps[:, L1_AT[s] % 2, :], scalar=0.0,
                                           in1=h_hi[:, n % 3, :].bitcast(F32), op0=ALU.max, op1=ALU.subtract).then_inc(h_lo_ready, 1)
                elif k == "OT":
                    dve.wait_ge(ot_filled, f + 1)
                    since(dve, out_stored, 16 * f)
                    v.tensor_copy(ob[:, :, :], pv_ps[:, :].rearrange("p (t d) -> p t d", t=T)).then_inc(ob_ready, 1)

            run(first[:6], one, 0, None)
            weights()
            run(first[6:], one, 0, None)
            run(STEPS, one, 1, 0)
            with dve.Fori(2, B) as b:
                run(STEPS, one, b, b - 1)
            run(last, one, None, B - 1)

        @block.tensor
        def _(pe):
            t = nc.tensor

            def weights():
                pe.wait_ge(b1_scaled, 1)
                for e in range(E):
                    pe.wait_ge(stage_loaded[e % 4], 16 * (e // 4 + 1))
                    if e >= 2:
                        pe.wait_ge(w1_centred, e - 1)
                    t.matmul(l1_ps[:, e % 2, :], mean_w[:, :], stage[:, e % 4, :], start=True, stop=False)
                    t.matmul(l1_ps[:, e % 2, :], pick_f[0:E, e // 2, e % 2, :], b1_s[:, :], start=False, stop=True).then_inc(w1_mean, 1)

            def turn(bank, src):
                for i in range(T):
                    last = t.transpose(bank[:, i * P:(i + 1) * P], src(i), ident[:, :])
                return last

            def one(s, b, f):
                k = s[0]
                if s in RING_AT:
                    bank_free(pe, RING_AT, s, b)
                    bank = ring[:, RING_AT[s] % 2, :]
                elif s in L1_AT:
                    bank_free(pe, L1_AT, s, f)
                    bank = l1_ps[:, L1_AT[s] % 2, :]
                if k == "YT":
                    if isinstance(b, int):
                        pe.wait_ge(consts_built, 1)
                        pe.wait_ge(consts_loaded, 16 * 9)
                    pe.wait_ge(xn_ready, b + 1)
                    turn(bank, lambda i: yn[:, i, :]).then_inc(ring_filled, 1)
                elif k == "PJ":
                    i = s[1]
                    pe.wait_ge(y_t_ready, b + 1)
                    t.matmul(bank[:, 0:3 * P], y_t[:, i * P:(i + 1) * P], wqkv_s[:, :], start=True, stop=True).then_inc(ring_filled, 1)
                elif k in ("KT", "QT"):
                    g = s[1]
                    pe.wait_ge(qk_lo_ready, T * b + T)
                    pe.wait_ge(m_cleared, b + 1)
                    which = 1 if k == "KT" else 0
                    turn(bank, lambda i: qk[:, i, which, HG * g:HG * g + HG, :].rearrange("p h r -> p (h r)")).then_inc(ring_filled, 1)
                elif k == "QM":
                    g = s[1]
                    pe.wait_ge(m_ready, HG * b + g + 1)
                    turn(bank, lambda i: qk[:, i, 0, HG * g:HG * g + HG, :].rearrange("p h r -> p (h r)")).then_inc(ring_filled, 1)
                elif k == "MX":
                    g, u = s[1], s[2]
                    pair, v, head = unit(g, u)
                    pe.wait_ge(kz_ready, HEADS * b + HG * g + HG)
                    pe.wait_ge(q1_ready, HG * b + g + 1)

                    def rows(i, head, at):
                        n = (i + 1) * P
                        t.matmul(bank[:, at:at + n], q1[:, g % 2, i * P:(i + 1) * P], kz[:, g % 2, head, 0:n], start=True, stop=False)
                        return t.matmul(bank[:, at + n - P:at + n], ident_b[:, :], causal[:, :], start=False, stop=True)

                    if v in (0, 2):
                        last = rows(3, head, 0)
                    elif v in (1, 3):
                        rows(2, head, 0)
                        last = rows(0, head, 3 * P)
                    else:
                        rows(1, 2 * pair, 0)
                        last = rows(1, 2 * pair + 1, 2 * P)
                    last.then_inc(ring_filled, 1)
                elif k == "ST":
                    g, u = s[1], s[2]
                    pair, v, head = unit(g, u)
                    n = 10 * g + u
                    since(pe, exp_ready, 40 * b + n - 1)
                    pe.wait_ge(q2_ready, HG * b + g + 1)
                    st = st_ps[:, n % 2, :]

                    def cols(j, head, lo, hi, at):
                        return t.matmul(st[:, at:at + (hi - lo) * P], kz[:, g % 2, head, j * P:(j + 1) * P],
                                        q2[:, g % 2, lo * P:hi * P], start=True, stop=True)

                    if v in (0, 2):
                        for j in range(T):
                            last = cols(j, head, j, j + 1, j * P)
                    elif v in (1, 3):
                        cols(0, head, 1, 4, 0)
                        last = cols(2, head, 3, 4, 3 * P)
                    else:
                        cols(1, 2 * pair, 2, 4, 0)
                        last = cols(1, 2 * pair + 1, 2, 4, 2 * P)
                    last.then_inc(st_filled, 1)
                elif k == "PV":
                    h = s[1]
                    pe.wait_ge(p_lo_ready, HEADS * b + h + 1)
                    if h == 0:
                        pe.wait_ge(v3_ready, b + 1)
                        since(pe, ob_ready, b - 1)
                    if h % HG == 0:
                        since(pe, pv_read, HG * b + h // HG)
                    at = {(j, j): j for j in range(T)}
                    at.update({(0, 1): 4, (0, 2): 5, (0, 3): 6, (2, 3): 7, (1, 2): 8, (1, 3): 9})
                    for i in range(T):
                        o = pv_ps[:, (HG * i + h % HG) * VW:(HG * i + h % HG) * VW + 3 * HD + 1]
                        for j in range(i + 1):
                            c = at[(j, i)] * P
                            rhs = v_op[:, j, h, 0:3 * HD + 1]
                            t.matmul(o, p_hi[:, h % 4, c:c + P], rhs, start=(j == 0), stop=False)
                            last = t.matmul(o, p_lo[:, h % 4, c:c + P], rhs, start=False, stop=(j == i))
                    last.then_inc(pv_done, 1)
                elif k == "AT":
                    pe.wait_ge(attn_ready, HG * b + HG)
                    turn(bank, lambda i: attn[:, i, :, :].rearrange("p h e -> p (h e)")).then_inc(ring_filled, 1)
                elif k == "WO":
                    pe.wait_ge(a_t_ready, b + 1)
                    for i in range(T):
                        last = t.matmul(bank[:, i * P:(i + 1) * P], a_t[:, i * P:(i + 1) * P], wo_s[:, :], start=True, stop=True)
                    last.then_inc(ring_filled, 1)
                elif k == "X2T":
                    pe.wait_ge(xn2_ready, b + 1)
                    turn(bank, lambda i: xn2[:, i, :]).then_inc(ring_filled, 1)
                elif k == "GT":
                    pe.wait_ge(x2_t_ready, b + 1)
                    for i in range(T):
                        last = t.matmul(bank[:, i * E:(i + 1) * E], x2_t[:, i * P:(i + 1) * P], wg_s[:, :], start=True, stop=True)
                    last.then_inc(ring_filled, 1)
                elif k == "MKT":
                    pe.wait_ge(m_tok_ready, b + 1)
                    turn(bank, lambda i: m_tok[:, i, :]).then_inc(ring_filled, 1)
                elif k == "XE":
                    e = s[1]
                    pe.wait_ge(m_t_ready, f + 1)
                    pe.wait_ge(pick_ready, 1)
                    t.matmul(bank[:, :], pick[:, e, :], m_t[:, :], start=True, stop=True).then_inc(l1_filled, 1)
                elif k == "ACC0":
                    since(pe, acc_saved, f)
                    pe.wait_ge(m_t_ready, f + 1)
                    pe.wait_ge(x1_ready, f + 1)
                    pe.wait_ge(b2_hi_ready, 2)
                    t.matmul(acc_ps[:, :], b2_x[:, :], m_t[:, :], start=True, stop=False)
                    for i in range(T):
                        last = t.matmul(acc_ps[:, i * P:(i + 1) * P], x1[:, i, :], ident[:, :], start=False, stop=False)
                    last.then_inc(acc_begun, 1)
                elif k == "L1":
                    n = s[1]
                    e, c = n // C, n % C
                    if c == 0:
                        pe.wait_ge(xe_lo_ready, E * f + e + 1)
                        pe.wait_ge(w_lo_ready, 2 * E)
                    w = slice(c * P, c * P + P)
                    t.matmul(bank, w1_lo[:, e, w], xe_hi[:, e % 2, :], start=True, stop=False)
                    t.matmul(bank, w1_hi[:, e, w], xe_lo[:, e % 2, :], start=False, stop=False)
                    t.matmul(bank, w1_hi[:, e, w], xe_hi[:, e % 2, :], start=False, stop=True).then_inc(l1_filled, 1)
                elif k == "L2":
                    n = s[1]
                    pe.wait_ge(h_lo_ready, N1 * f + n + 1)
                    t.matmul(acc_ps[:, :], w2_lo[:, n, :], h_hi[:, n % 3, :], start=False, stop=False)
                    t.matmul(acc_ps[:, :], w2_hi[:, n, :], h_lo[:, n % 3, :], start=False, stop=False)
                    t.matmul(acc_ps[:, :], w2_hi[:, n, :], h_hi[:, n % 3, :], start=False, stop=(n == N1 - 1)).then_inc(l2_done, 1)
                elif k == "OT":
                    pe.wait_ge(acc_saved, f + 1)
                    pe.wait_ge(pv_read, HG * B if b is None else HG * b + HG)
                    since(pe, ob_ready, f)
                    turn(pv_ps, lambda i: acc_s[:, i * P:(i + 1) * P]).then_inc(ot_filled, 1)

            run(first[:6], one, 0, None)
            weights()
            run(first[6:], one, 0, None)
            run(STEPS, one, 1, 0)
            with pe.Fori(2, B) as b:
                run(STEPS, one, b, b - 1)
            run(last, one, None, B - 1)


_INS = ["x", "ln_w", "ln_b", "wqkv", "wo", "w_gate", "w1", "b1", "w2", "b2"]


def kernel(L0_attn_x, L0_attn_ln_w, L0_attn_ln_b, L0_attn_wq, L0_attn_wk, L0_attn_wv, L0_attn_wo,
           L0_ffn_W_gate, L0_ffn_W1, L0_ffn_b1, L0_ffn_W2, L0_ffn_b2):
    import numpy as _np
    import concourse.bacc as _bacc
    from concourse import mybir as _mybir
    from concourse.bass_utils import run_bass_kernel_spmd as _run

    def by_input(w):
        return _np.transpose(_np.asarray(w), (1, 0, 2)).reshape(w.shape[1], -1)

    wqkv = _np.concatenate([by_input(w) for w in (L0_attn_wq, L0_attn_wk, L0_attn_wv)], axis=1)
    given = [L0_attn_x, L0_attn_ln_w, L0_attn_ln_b, wqkv, L0_attn_wo, L0_ffn_W_gate, L0_ffn_W1, L0_ffn_b1, L0_ffn_W2, L0_ffn_b2]
    nc = _bacc.Bacc("TRN2", target_bir_lowering=False, num_devices=1)
    arrays, args = {}, []
    for name, a in zip(_INS, given):
        a = _np.ascontiguousarray(a)
        arrays[f"in_{name}_dram"] = a
        args.append(nc.dram_tensor(f"in_{name}_dram", a.shape, _mybir.dt.from_np(a.dtype), kind="ExternalInput").ap())
    out = nc.dram_tensor("out_dram", arrays["in_x_dram"].shape, _mybir.dt.float32, kind="ExternalOutput").ap()
    moe_block_kernel(nc, *args, out)
    r = _run(nc, [arrays], core_ids=[0])
    return r.results[0]["out_dram"]
```

```python
from contextlib import ExitStack

import concourse.bass as bass
from concourse import mybir

P = 128
F32 = mybir.dt.float32
F32R = mybir.dt.float32r
F16 = mybir.dt.float16
BF16 = mybir.dt.bfloat16
ALU = mybir.AluOpType
ACT = mybir.ActivationFunctionType
X = mybir.AxisListType.X
EPS = 1e-5
MASKED = -1e30
UNITS = 10


TIMES = {
    "group": 12.05, "start": 1.7, "KT": -2.14, "QT": -6.02, "QM": -1.36, "NM": 0.13, "ST": 0.18, "PM0": -0.43,
    "PM1": -0.16, "PH0": 1.91, "PH1": 2.74, "LO0": 1.47, "LO1": 2.18, "PV0": 6.04, "PV1": 7.11, "ON": 1.5,
    "LN1": 29.68, "YN": 32.54, "YT": 32.32, "PJ": 37.4, "PJ_step": 0.58, "QC": 41.02, "KT'": 40.06,
    "QT'": 40.58, "MX'": 42.89, "NM'": 2.67, "AT": -0.22, "WO": 0.41, "X2N": 1.1, "X2T": 2.89, "VS": 13.81,
    "GT": 5.83, "GE": 4.31, "XN": 0.4, "MKT": 14.26, "L2": 2.71, "XE": -4.21, "ACC0": -0.26, "W": 1.84,
    "OA": 6.15, "OT": 7.1,
}
EXPERTS = [1.63, 8.91, 13.38, 21.72, 30.0, 37.55, 46.08, 49.97, 55.33]
LATE = {
    "scalar": {"ST": 0.02, "PJ": 0.06, "X2T": -0.21, "MKT": 8.56, "YT": -1.21, "QM": 0.66, "KT": 0.29, "XE": 0.71, "VS": -0.0, "AT": 2.37, "QT": 0.13, "L1": -0.08},
    "vector": {"L1": 0.91, "XE": -0.09, "YN": -0.94, "LN1": -2.93, "OT": 2.61, "MX": 0.12, "XN": 1.96, "X2N": 1.67, "PJ": 0.86, "GT": -2.98, "NM": 0.17, "GE": 1.36, "ON": -0.89, "WO": 0.48, "VS": 2.63},
    "gpsimd": {"XE": 0.72, "XN": 1.32, "LN1": -2.28, "VS": 1.4, "WO": 0.6, "QC": -0.48},
    "tensor": {},
}


def schedule(batch=True, ahead=True, beside=None):
    t, steps = TIMES, []

    def add(time, *step):
        if batch:
            steps.append((time, step))

    def add_next(time, *step):
        if ahead:
            steps.append((time, step + ("next",)))

    def unit_time(n):
        return t["group"] * (n // UNITS) + t["start"] + n % UNITS

    for g in range(4):
        begin = unit_time(UNITS * g)
        if g < 3:
            add(begin + t["KT"], "KT", g + 1)
            add(begin + t["QT"], "QT", g + 1)
        add(begin + t["QM"], "QM", g)
        for u in range(UNITS):
            if g < 3:
                add(begin + u, "MX", g + 1, u)
            add(begin + u + t["ST"], "ST", g, u)
        if g < 3:
            add(begin + UNITS - 1 + t["NM"], "NM", g + 1)
    for h in range(16):
        ready, second = unit_time(5 * (h // 2) + 4), str(h % 2)
        for k in ("PM", "PH", "LO"):
            add(ready + t[k + second], k, h)
        pv = ready + t["PV" + second]
        add(pv, "PV", h)
        if h % 4 == 3:
            add(pv + t["ON"], "ON", h // 4)
    done = unit_time(39) + t["PV1"] + t["ON"]
    for k in ("AT", "WO", "X2N", "X2T", "GT", "GE", "MKT"):
        add(done + t[k], k)
    for k in ("VS", "XN"):
        add_next(done + t[k], k)
    for k in ("LN1", "YN", "YT", "QC"):
        add_next(t[k], k)
    for i in range(4):
        add_next(t["PJ"] + i * t["PJ_step"], "PJ", i)
    add_next(t["KT'"], "KT", 0)
    add_next(t["QT'"], "QT", 0)
    for u in range(UNITS):
        add_next(t["MX'"] + u, "MX", 0, u)
    add_next(t["MX'"] + UNITS - 1 + t["NM'"], "NM", 0)
    if beside == "weights":
        steps.append((-10.0, ("WB",)))
        for n in range(16):
            steps.append((t["W"] * n, ("W", n)))
    elif beside == "ffn":
        steps.append((t["ACC0"], ("ACC0",)))
        for n in range(32):
            e = n // 4
            time = EXPERTS[e] + (n % 4) * (EXPERTS[e + 1] - EXPERTS[e]) / 4
            if n % 4 == 0:
                steps.append((time + t["XE"], ("XE", n // 4)))
            steps.append((time, ("L1", n)))
            steps.append((time + t["L2"], ("L2", n)))
        steps.append((time + t["L2"] + t["OA"], ("OA",)))
        steps.append((time + t["L2"] + t["OT"], ("OT",)))
    return steps


def order(steps, engine):
    late = LATE[engine]
    result = [s for _, s in sorted(steps, key=lambda x: x[0] + late.get(x[1][0], 0.0))]
    for kind in {s[0] for s in result}:
        for ahead in (False, True):
            same = [s for s in result if s[0] == kind and (s[-1] == "next") == ahead]
            assert same == sorted(same)
    return result


AHEAD = schedule(batch=False)
FIRST = schedule(beside="weights")
STEPS = schedule(beside="ffn")
LAST = schedule(ahead=False, beside="ffn")
FFN_ONLY = schedule(batch=False, ahead=False, beside="ffn")
RING_STEPS = ("YT", "PJ", "KT", "QT", "MX", "QM", "AT", "WO", "X2T", "GT", "MKT")


def ring_users(steps):
    return [s for s in order(steps, "tensor") if s[0] in RING_STEPS]


RING = len(ring_users(STEPS))
RING_AHEAD = len(ring_users(AHEAD))
L1_AT = {s: n for n, s in enumerate([s for s in order(STEPS, "tensor") if s[0] in ("XE", "L1")])}
L1_USES = len(L1_AT)
assert RING % 2 == 0 and L1_USES % 2 == 0


class Pass:

    def __init__(self, steps, before, start):
        self.steps = {engine: order(steps, engine) for engine in LATE}
        self.start = start
        self.users = (ring_users(before) if before else [None, None])[-2:] + ring_users(steps)
        self.at = {s: n for n, s in enumerate(ring_users(steps))}


def moe_block_kernel(nc, x, ln_w, ln_b, wqkv, wo, w_gate, w1, b1, w2, b2, out):
    B, S, D = x.shape
    E, _, H = w1.shape
    T = S // P
    HEADS, HD = 16, 8
    HG = 4
    R = 32
    C = H // P
    N1 = E * C
    BLK = 10
    SCALE = float(HD) ** -0.5
    VW = 32

    x_t = x.rearrange("b (t p) d -> b p t d", p=P)
    out_t = out.rearrange("b (t p) d -> b p t d", p=P)
    w1_t = w1.rearrange("e d h -> d e h")
    w2_t = w2.rearrange("e (c p) d -> p e c d", p=P)

    with ExitStack() as ctx:
        def sb(name, shape, dt=F32):
            return ctx.enter_context(nc.sbuf_tensor(name, shape, dt))

        def sem(name):
            return ctx.enter_context(nc.semaphore(name))

        ring = ctx.enter_context(nc.psum_tensor("ring", [P, 2, 512], F32))
        st_ps = ctx.enter_context(nc.psum_tensor("st_ps", [P, 2, 512], F32))
        l1_ps = ctx.enter_context(nc.psum_tensor("l1_ps", [P, 2, 512], F32))
        acc_ps = ctx.enter_context(nc.psum_tensor("acc_ps", [P, 512], F32))
        pv_ps = ctx.enter_context(nc.psum_tensor("pv_ps", [P, 512], F32))

        ident = sb("ident", [P, P])
        ident_b = sb("ident_b", [P, P], BF16)
        causal = sb("causal", [P, P], BF16)
        pick = sb("pick", [P, E, P], F32R)
        half_neg = sb("half_neg", [P, T])
        eps = sb("eps", [P, T])
        lnw = sb("lnw", [P, 1])
        lnb = sb("lnb", [P, 1])
        wqkv_s = sb("wqkv_s", [P, 3 * P])
        wo_s = sb("wo_s", [P, D])
        wg_s = sb("wg_s", [P, E])
        b1_s = sb("b1_s", [E, H])
        b2_x = sb("b2_x", [P, D], F32R)
        w1_hi = sb("w1_hi", [P, E, H], F32R)
        w1_lo = sb("w1_lo", [P, E, H], F32R)
        w2_hi = sb("w2_hi", [P, N1, D], F32R)
        w2_lo = sb("w2_lo", [P, N1, D], F32R)
        xb = sb("xb", [P, T, D])
        stats = sb("stats", [P, T, 6])
        mv = sb("mv", [P, T, 2])
        rs = sb("rs", [P, 6, T])
        stats2 = sb("stats2", [P, T, 6])
        mv2 = sb("mv2", [P, T, 2])
        rs2 = sb("rs2", [P, 2, T])
        yn = sb("yn", [P, T, D])
        xn = sb("xn", [P, T, D])
        xr = xn
        y_t = sb("y_t", [P, S])
        qk = sb("qk", [P, T, 2, HEADS, R])
        vr = sb("vr", [P, T, HEADS, HD])
        v_op = sb("v_op", [P, T, HEADS, VW], BF16)
        kz = sb("kz", [P, 2, HG, S], F32R)
        q1 = sb("q1", [P, 2, S], F32R)
        q2 = sb("q2", [P, 2, S], F32R)
        bmax = sb("bmax", [P, HEADS, BLK])
        nmax = sb("nmax", [P, T, HG])
        p32 = sb("p32", [P, 4, BLK * P])
        p_hi = sb("p_hi", [P, 4, BLK * P], F16)
        p_lo = sb("p_lo", [P, 4, BLK * P], F16)
        osum = sb("osum", [P, T * HG, HD])
        rden = sb("rden", [P, T * HG])
        attn = sb("attn", [P, T, HEADS, HD])
        a_t = y_t
        x1 = sb("x1", [P, T, D])
        xn2 = yn
        x2_t = sb("x2_t", [P, S])
        gate = sb("gate", [P, T, E])
        top = sb("top", [P, T, 8])
        gsel = sb("gsel", [P, T, E])
        gexp = sb("gexp", [P, T, E])
        gsum = sb("gsum", [P, T])
        m_tok = sb("m_tok", [P, T, P])
        m_t = sb("m_t", [P, S], F32R)
        xe = sb("xe", [P, 2, S])
        xe_hi = sb("xe_hi", [P, 2, S], F32R)
        xe_lo = sb("xe_lo", [P, 2, S], F32R)
        h_hi = sb("h_hi", [P, 3, S], F32R)
        h_lo = sb("h_lo", [P, 3, S], F32R)
        acc_s = sb("acc_s", [P, S])
        ob = sb("ob", [P, T, D])
        stage = [acc_s[:, :], ob[:, :, :].rearrange("p t d -> p (t d)"), x2_t[:, :], x1[:, :, :].rearrange("p t d -> p (t d)")]
        STAGES = len(stage)
        pick_f = xe[:, :, :].rearrange("p a s -> p (a s)").rearrange("p (a b k) -> p a b k", b=2, k=P)
        w1c = xe
        mean_w = m_tok[:, 0, :]
        b2_f = m_tok[:, 1, :]

        consts_loaded = sem("consts_loaded")
        stage_loaded = [sem(f"stage_loaded{k}") for k in range(STAGES)]
        x_loaded = sem("x_loaded")
        out_stored = sem("out_stored")
        waited_apart = sem("waited_apart")
        tables_set = sem("tables_set")
        dve_set = sem("dve_set")
        qk_cleared = sem("qk_cleared")
        kz_cleared = sem("kz_cleared")
        picks_set = sem("picks_set")
        m_tok_cleared = sem("m_tok_cleared")
        b2_f_cleared = sem("b2_f_cleared")
        norm_loaded = sem("norm_loaded")
        wqkv_loaded = sem("wqkv_loaded")
        consts_built = sem("consts_built")
        b1_scaled = sem("b1_scaled")
        w1_mean = sem("w1_mean")
        w1_centred = sem("w1_centred")
        w_hi_ready = sem("w_hi_ready")
        w_lo_ready = sem("w_lo_ready")
        b2_hi_ready = sem("b2_hi_ready")
        pick_ready = sem("pick_ready")
        stats_ready = sem("stats_ready")
        rs_step = sem("rs_step")
        stats2_ready = sem("stats2_ready")
        rs2_step = sem("rs2_step")
        yn_ready = sem("yn_ready")
        v_raw_ready = sem("v_raw_ready")
        rstd_ready = sem("rstd_ready")
        xn_ready = sem("xn_ready")
        xr_ready = sem("xr_ready")
        ring_filled = sem("ring_filled")
        y_t_ready = sem("y_t_ready")
        qk_hi_ready = sem("qk_hi_ready")
        qk_lo_ready = sem("qk_lo_ready")
        v1_ready = sem("v1_ready")
        v_rest_ready = sem("v_rest_ready")
        v2_ready = sem("v2_ready")
        v3_ready = sem("v3_ready")
        kz_ready = sem("kz_ready")
        q1_ready = sem("q1_ready")
        q2_ready = sem("q2_ready")
        bmax_ready = sem("bmax_ready")
        nmax_ready = sem("nmax_ready")
        m_cleared = sem("m_cleared")
        m_hi_ready = sem("m_hi_ready")
        m_ready = sem("m_ready")
        st_filled = sem("st_filled")
        exp_ready = sem("exp_ready")
        p_masked = sem("p_masked")
        p_hi_ready = sem("p_hi_ready")
        p_lo_ready = sem("p_lo_ready")
        pv_done = sem("pv_done")
        osum_ready = sem("osum_ready")
        pv_read = sem("pv_read")
        attn_ready = sem("attn_ready")
        a_t_ready = sem("a_t_ready")
        x1_ready = sem("x1_ready")
        xn2_ready = sem("xn2_ready")
        x2_t_ready = sem("x2_t_ready")
        gate_step = sem("gate_step")
        gexp_ready = sem("gexp_ready")
        m_tok_ready = sem("m_tok_ready")
        m_t_ready = sem("m_t_ready")
        xe_ready = sem("xe_ready")
        xe_hi_ready = sem("xe_hi_ready")
        xe_lo_ready = sem("xe_lo_ready")
        acc_begun = sem("acc_begun")
        l1_filled = sem("l1_filled")
        h_hi_ready = sem("h_hi_ready")
        h_lo_ready = sem("h_lo_ready")
        l2_done = sem("l2_done")
        acc_saved = sem("acc_saved")
        ot_filled = sem("ot_filled")
        ob_ready = sem("ob_ready")

        def batch_of(step, b):
            return b + 1 if step[-1] == "next" else b

        def after_next(b):
            return min(b + 2, B) if isinstance(b, int) else b + 2

        CONSTS = 6

        def since(eng, signal, value):
            if not (isinstance(value, int) and value <= 0):
                eng.wait_ge(signal, value)

        def read_by(step, b):
            k, g = step[0], (step[1] if len(step) > 1 else 0)
            b = batch_of(step, b)
            return {
                "YT": lambda: (y_t_ready, b + 1),
                "PJ": lambda: (qk_lo_ready, T * b + g + 1),
                "KT": lambda: (kz_ready, HEADS * b + HG * g + HG),
                "QT": lambda: (q1_ready, HG * b + g + 1),
                "QM": lambda: (q2_ready, HG * b + g + 1),
                "MX": lambda: (bmax_ready, 40 * b + UNITS * g + step[2] + 1),
                "AT": lambda: (a_t_ready, b + 1),
                "WO": lambda: (x1_ready, b + 1),
                "X2T": lambda: (x2_t_ready, b + 1),
                "GT": lambda: (gate_step, 8 * b + 1),
                "MKT": lambda: (m_t_ready, b + 1),
                "XE": lambda: (xe_ready, E * b + g + 1),
                "L1": lambda: (h_lo_ready, N1 * b + g + 1),
            }[k]()

        def apart(eng):
            eng.sem_inc(waited_apart, 1)

        def ring_bank(p, step):
            return ring[:, (p.start + p.at[step]) % 2, :]

        def ring_free(eng, p, step, b):
            n = p.at[step]
            if p.users[n] is not None:
                eng.wait_ge(*read_by(p.users[n], b - 1 if n < 2 else b))

        def ring_full(eng, p, step, b):
            eng.wait_ge(ring_filled, RING * b + p.start + p.at[step] + 1)

        def l1_free(eng, step, f):
            users = list(L1_AT)
            n = L1_AT[step] - 2
            if n >= 0:
                eng.wait_ge(*read_by(users[n], f))
            else:
                signal, value = read_by(users[n], f - 1)
                since(eng, signal, value)

        def unit(g, u):
            pair, v = u // 5, u % 5
            head = 2 * pair + (1 if v in (2, 3) else 0)
            return pair, v, head

        before_first = Pass(AHEAD, None, RING)
        first = Pass(FIRST, AHEAD, RING_AHEAD)
        second = Pass(STEPS, FIRST, RING_AHEAD)
        middle = Pass(STEPS, STEPS, RING_AHEAD)
        last = Pass(LAST, STEPS, RING_AHEAD)
        ffn_only = Pass(FFN_ONLY, None, 0)

        def all_passes(eng, name, one):

            def run(p, b):
                for s in p.steps[name]:
                    one(p, s, b, batch_of(s, b), b - 1)

            run(before_first, -1)
            run(first, 0)
            run(second, 1)
            with eng.Fori(2, B - 1) as b:
                run(middle, b)
            run(last, B - 1)
            run(ffn_only, B)

        block = ctx.enter_context(nc.Block())

        @block.sync
        def _(sp):
            sp.dma_start(xb[:, :, :], x_t[0]).then_inc(x_loaded, 16)
            sp.dma_start(lnw[:, :], ln_w.rearrange("(d a) -> d a", a=1)).then_inc(norm_loaded, 16)
            sp.dma_start(lnb[:, :], ln_b.rearrange("(d a) -> d a", a=1)).then_inc(norm_loaded, 16)
            sp.dma_start(wqkv_s[:, :], wqkv).then_inc(wqkv_loaded, 16)
            for dst, src in ((wo_s, wo), (wg_s, w_gate), (b1_s, b1)):
                sp.dma_start(dst[:, :], src).then_inc(consts_loaded, 16)
            sp.wait_ge(b2_f_cleared, 1)
            for k in range(3):
                sp.dma_start(b2_f[32 * k:32 * k + E, :], b2).then_inc(consts_loaded, 16)
            for n in range(2 * E):
                e = n % E
                if n >= STAGES:
                    sp.wait_ge(w_lo_ready, n - STAGES + 1)
                src = w1_t[:, e, :] if n < E else w2_t[:, e, :, :]
                dst = stage[n % STAGES] if n < E else stage[n % STAGES].rearrange("p (c d) -> p c d", c=C)
                sp.dma_start(dst, src).then_inc(stage_loaded[n % STAGES], 16)

            def load(b, src):
                sp.wait_ge(xr_ready, b + 1)
                sp.dma_start(xb[:, :, :], src).then_inc(x_loaded, 16)

            def store(f, dst):
                sp.wait_ge(ob_ready, f + 1)
                sp.dma_start(dst, ob[:, :, :]).then_inc(out_stored, 16)

            load(0, x_t[1])
            load(1, x_t[2])
            with sp.Fori(2, B - 1) as b:
                store(b - 2, out_t[bass.ds(b - 2, 1)].rearrange("a p t d -> p (a t) d"))
                load(b, x_t[bass.ds(b + 1, 1)].rearrange("a p t d -> p (a t) d"))
            store(B - 3, out_t[B - 3])
            store(B - 2, out_t[B - 2])
            store(B - 1, out_t[B - 1])
            sp.wait_ge(out_stored, 16 * B)

        @block.gpsimd
        def _(pool):
            g = nc.gpsimd
            g.memset(ident[:, :], 0.0)
            g.memset(causal[:, :], 0.0)
            g.memset(half_neg[:, :], -0.5)
            g.memset(eps[:, :], EPS).then_inc(tables_set, 1)
            pool.wait_ge(tables_set, 1)
            g.affine_select(out=ident[:, :], in_=ident[:, :], compare_op=ALU.not_equal, fill=1.0, base=0,
                            pattern=[[-1, P]], channel_multiplier=1)
            g.affine_select(out=causal[:, :], in_=causal[:, :], compare_op=ALU.is_ge, fill=MASKED, base=0,
                            pattern=[[-1, P]], channel_multiplier=1).then_inc(tables_set, 1)
            pool.wait_ge(tables_set, 2)
            g.tensor_copy(ident_b[:, :], ident[:, :]).then_inc(consts_built, 1)

            def power(dst, src, n):
                pool.wait_ge(rs_step, n)
                return g.tensor_tensor(dst, src, half_neg[:, :], ALU.pow)

            def one(p, s, c, b, f):
                k = s[0]
                if k == "LN1":
                    pool.wait_ge(stats_ready, 2 * b + 2)
                    z = 6 * b
                    g.tensor_tensor(rs[:, 0, :], mv[:, :, 1], eps[:, :], ALU.add).then_inc(rs_step, 1)
                    power(rs[:, 1, :], rs[:, 0, :], z + 1).then_inc(rs_step, 1)
                    pool.wait_ge(rs_step, z + 2)
                    g.tensor_tensor(rs[:, 2, :], rs[:, 1, :], mv[:, :, 1], ALU.mult).then_inc(rs_step, 1)
                    pool.wait_ge(rs_step, z + 3)
                    g.tensor_tensor(rs[:, 3, :], rs[:, 2, :], rs[:, 1, :], ALU.mult).then_inc(rs_step, 1)
                    pool.wait_ge(rs_step, z + 4)
                    g.tensor_tensor(rs[:, 4, :], rs[:, 3, :], eps[:, :], ALU.add).then_inc(rs_step, 1)
                    power(rs[:, 5, :], rs[:, 4, :], z + 5).then_inc(rs_step, 1)
                    pool.wait_ge(rs_step, z + 6)
                    g.tensor_tensor(rs[:, 0, :], rs[:, 5, :], rs[:, 1, :], ALU.mult).then_inc(rstd_ready, 1)
                elif k == "XN":
                    pool.wait_ge(xn_ready, b + 1)
                    g.tensor_tensor(xr[:, :, :], xb[:, :, :], xn[:, :, :], ALU.add).then_inc(xr_ready, 1)
                elif k == "QC":
                    if isinstance(b, int) and b == 0:
                        pool.wait_ge(qk_cleared, 1)
                    since(pool, q2_ready, HG * b)
                    apart(pool)
                    g.memset(qk[:, :, 0, :, 3 * HD:3 * HD + 2], 0.0).then_inc(m_cleared, 1)
                elif k == "VS":
                    pool.wait_ge(v2_ready, b + 1)
                    g.tensor_tensor(v_op[:, :, :, 2 * HD:3 * HD], vr[:, :, :, :], v_op[:, :, :, HD:2 * HD],
                                    ALU.subtract).then_inc(v3_ready, 1)
                elif k == "PM":
                    h = s[1]
                    pool.wait_ge(exp_ready, 40 * b + 10 * (h // 4) + 5 * (h % 4 // 2) + 5)
                    apart(pool)
                    v = p32[:, h % 4, 0:T * P].rearrange("p (t s) -> p t s", t=T)
                    g.affine_select(out=v, in_=v, compare_op=ALU.is_ge, fill=0.0, base=0,
                                    pattern=[[0, T], [1, P]], channel_multiplier=-1).then_inc(p_masked, 1)
                elif k == "LO":
                    h = s[1]
                    pool.wait_ge(p_hi_ready, HEADS * b + h + 1)
                    since(pool, pv_done, HEADS * b + h - 3)
                    g.tensor_tensor(p_lo[:, h % 4, :], p32[:, h % 4, :], p_hi[:, h % 4, :], ALU.subtract).then_inc(p_lo_ready, 1)
                elif k == "WO":
                    pool.wait_ge(stats2_ready, 2 * b + 2)
                    g.tensor_tensor(rs2[:, 0, :], mv2[:, :, 1], eps[:, :], ALU.add).then_inc(rs2_step, 1)
                    pool.wait_ge(rs2_step, 2 * b + 1)
                    g.tensor_tensor(rs2[:, 1, :], rs2[:, 0, :], half_neg[:, :], ALU.pow).then_inc(rs2_step, 1)
                elif k == "XE":
                    e = s[1]
                    pool.wait_ge(xe_hi_ready, E * f + e + 1)
                    g.tensor_tensor(xe_lo[:, e % 2, :], xe[:, e % 2, :], xe_hi[:, e % 2, :].bitcast(F32), ALU.subtract).then_inc(xe_lo_ready, 1)
                elif k == "WB":
                    g.memset(b2_f, 0.0).then_inc(b2_f_cleared, 1)
                    g.memset(mean_w, 1.0 / D)
                    g.memset(pick_f, 0.0).then_inc(picks_set, 1)
                    pool.wait_ge(picks_set, 1)
                    g.affine_select(out=pick_f, in_=pick_f, compare_op=ALU.not_equal, fill=1.0, base=0,
                                    pattern=[[-2, 4], [-1, 2], [0, P]], channel_multiplier=1).then_inc(picks_set, 1)
                    pool.wait_ge(picks_set, 2)
                    g.affine_select(out=pick_f, in_=pick_f, compare_op=ALU.not_equal, fill=1.0, base=-32,
                                    pattern=[[-2, 4], [-1, 2], [0, P]], channel_multiplier=1).then_inc(picks_set, 1)
                elif k == "W":
                    n, e = s[1], s[1] % E
                    if n == 2 * E - 1:
                        pool.wait_ge(w1_mean, E)
                        pool.wait_ge(b2_hi_ready, 2)
                        g.memset(m_tok[:, :, :], 0.0).then_inc(m_tok_cleared, 1)
                    pool.wait_ge(w_hi_ready, n + 1)
                    if n < E:
                        g.tensor_tensor(w1_lo[:, e, :], w1c[:, n % 2, :], w1_hi[:, e, :].bitcast(F32), ALU.subtract).then_inc(w_lo_ready, 1)
                    else:
                        g.tensor_tensor(w2_lo[:, C * e:C * e + C, :], stage[n % STAGES].rearrange("p (c d) -> p c d", c=C),
                                        w2_hi[:, C * e:C * e + C, :].bitcast(F32), ALU.subtract).then_inc(w_lo_ready, 1)

            all_passes(pool, "gpsimd", one)

        @block.scalar
        def _(act):
            a = nc.scalar
            copy = ACT.Copy

            def one(p, s, c, b, f):
                k = s[0]
                bank = ring_bank(p, s) if k in RING_STEPS else None
                if k == "YT":
                    ring_full(act, p, s, c)
                    if isinstance(b, int):
                        act.wait_ge(norm_loaded, 16 * 2)
                    since(act, x1_ready, b - 1)
                    a.activation(y_t[:, :], bank[:, :], ACT.Identity, bias=lnb[:, 0:1], scale=lnw[:, 0:1]).then_inc(y_t_ready, 1)
                elif k == "PJ":
                    i = s[1]
                    ring_full(act, p, s, c)
                    since(act, v3_ready, b)
                    a.activation(vr[:, i, :, :], bank[:, 2 * P:3 * P].rearrange("p (h e) -> p h e", e=HD), copy).then_inc(v_raw_ready, 1)
                    if isinstance(b, int) and b == 0:
                        act.wait_ge(qk_cleared, 1)
                    v = qk[:, i, :, :, 0:HD].rearrange("p k h e -> p (k h) e")
                    a.activation(v.bitcast(F32R), bank[:, 0:2 * P].rearrange("p (h e) -> p h e", e=HD),
                                 copy).then_inc(qk_hi_ready, 1)
                elif k == "VS":
                    act.wait_ge(v_raw_ready, T * b + T)
                    since(act, pv_done, HEADS * b)
                    a.activation(v_op[:, :, :, 0:HD], vr[:, :, :, :], copy).then_inc(v1_ready, 1)
                elif k == "KT":
                    g = s[1]
                    ring_full(act, p, s, c)
                    if isinstance(b, int):
                        act.wait_ge(kz_cleared, 1)
                    for hh in range(HG):
                        rows = slice(R * hh, R * hh + R)
                        a.activation(kz[rows, g % 2, hh, :], bank[rows, :], copy).then_inc(kz_ready, 1)
                elif k == "QT":
                    g = s[1]
                    ring_full(act, p, s, c)
                    a.activation(q1[:, g % 2, :], bank[:, :], copy).then_inc(q1_ready, 1)
                elif k == "QM":
                    g = s[1]
                    ring_full(act, p, s, c)
                    a.activation(q2[:, g % 2, :], bank[:, :], copy).then_inc(q2_ready, 1)
                elif k == "ST":
                    g, u = s[1], s[2]
                    pair, v, head = unit(g, u)
                    act.wait_ge(st_filled, 40 * b + 10 * g + u + 1)
                    since(act, p_lo_ready, HEADS * b + 4 * g + 2 * pair - 2)
                    slot = (4 * g + head) % 4
                    if v in (0, 2):
                        dst, src = p32[:, slot, 0:512], st_ps[:, (10 * g + u) % 2, :]
                    elif v in (1, 3):
                        dst, src = p32[:, slot, 512:1024], st_ps[:, (10 * g + u) % 2, :]
                    else:
                        dst = p32[:, 2 * pair:2 * pair + 2, 1024:1280]
                        src = st_ps[:, (10 * g + u) % 2, :].rearrange("p (h s) -> p h s", h=2)
                    a.activation(dst, src, ACT.Exp, scale=SCALE).then_inc(exp_ready, 1)
                elif k == "AT":
                    ring_full(act, p, s, c)
                    a.activation(a_t[:, :], bank[:, :], copy).then_inc(a_t_ready, 1)
                elif k == "X2T":
                    ring_full(act, p, s, c)
                    if isinstance(b, int):
                        act.wait_ge(w_lo_ready, 2 * E)
                    since(act, xe_ready, E * b)
                    a.activation(x2_t[:, :], bank[:, :], copy).then_inc(x2_t_ready, 1)
                elif k == "GE":
                    act.wait_ge(gate_step, 8 * b + 3)
                    a.activation(gexp[:, :, :], gate[:, :, :], ACT.Exp).then_inc(gexp_ready, 1)
                elif k == "MKT":
                    ring_full(act, p, s, c)
                    since(act, xe_ready, E * b)
                    a.activation(m_t[:, :], bank[:, :], copy).then_inc(m_t_ready, 1)
                elif k == "XE":
                    e = s[1]
                    act.wait_ge(xe_ready, E * f + e + 1)
                    a.activation(xe_hi[:, e % 2, :], xe[:, e % 2, :], copy).then_inc(xe_hi_ready, 1)
                elif k == "L1":
                    n = s[1]
                    act.wait_ge(l1_filled, L1_USES * f + L1_AT[s] + 1)
                    since(act, l2_done, N1 * f + max(n - 2, 0))
                    a.activation(h_hi[:, n % 3, :], l1_ps[:, L1_AT[s] % 2, :], ACT.Relu).then_inc(h_hi_ready, 1)
                elif k == "WB":
                    act.wait_ge(picks_set, 3)
                    a.activation(pick[:, :, :].rearrange("p (a b) k -> p a b k", b=2), pick_f, copy).then_inc(pick_ready, 1)
                    act.wait_ge(consts_loaded, 16 * CONSTS)
                    a.activation(b1_s[:, :], b1_s[:, :], copy, scale=-1.0 / D).then_inc(b1_scaled, 1)
                    a.activation(b2_x[:, :], b2_f, copy).then_inc(b2_hi_ready, 1)
                elif k == "W":
                    n, e = s[1], s[1] % E
                    if n < E:
                        act.wait_ge(w1_centred, n + 1)
                        a.activation(w1_hi[:, e, :], w1c[:, n % 2, :], copy).then_inc(w_hi_ready, 1)
                    else:
                        act.wait_ge(stage_loaded[n % STAGES], 16 * (n // STAGES + 1))
                        a.activation(w2_hi[:, C * e:C * e + C, :], stage[n % STAGES].rearrange("p (c d) -> p c d", c=C),
                                     copy).then_inc(w_hi_ready, 1)
                elif k == "OA":
                    act.wait_ge(l2_done, N1 * f + N1)
                    since(act, ot_filled, f)
                    a.activation(acc_s[:, :], acc_ps[:, :], copy).then_inc(acc_saved, 1)

            all_passes(act, "scalar", one)

        @block.vector
        def _(dve):
            v = nc.vector

            v.memset(qk[:, :, :, :, :], 0.0).then_inc(dve_set, 1)
            v.memset(kz[:, :, :, :].bitcast(F32), 0.0).then_inc(kz_cleared, 1)
            dve.wait_ge(dve_set, 1)
            v.memset(qk[:, :, 1, :, 3 * HD:3 * HD + 2], 1.0).then_inc(qk_cleared, 1)
            v.memset(v_op[:, :, :, 3 * HD:VW], 1.0)

            def norm_stats(src, stats, mv, ready, z):
                for i in range(T):
                    last = v.bn_stats(stats[:, i, :], src[:, i, :])
                last.then_inc(ready, 1)
                dve.wait_ge(ready, z + 1)
                apart(dve)
                for i in range(T):
                    last = v.bn_aggr(mv[:, i, :], stats[:, i, :])
                last.then_inc(ready, 1)

            def one(p, s, c, b, f):
                k = s[0]
                bank = ring_bank(p, s) if k in RING_STEPS else None
                if k == "LN1":
                    dve.wait_ge(x_loaded, 16 * b + 16)
                    norm_stats(xb, stats, mv, stats_ready, 2 * b)
                elif k == "YN":
                    dve.wait_ge(rstd_ready, b + 1)
                    since(dve, x2_t_ready, b - 1)
                    for i in range(T):
                        last = v.tensor_scalar(yn[:, i, :], xb[:, i, :], mv[:, i, 0:1], rs[:, 0, i:i + 1], ALU.subtract, ALU.mult)
                    last.then_inc(yn_ready, 1)
                elif k == "XN":
                    dve.wait_ge(rs_step, 6 * b + 6)
                    since(dve, x1_ready, b)
                    for i in range(T):
                        last = v.tensor_scalar(xn[:, i, :], xb[:, i, :], mv[:, i, 0:1], rs[:, 1, i:i + 1], ALU.subtract, ALU.mult)
                    last.then_inc(xn_ready, 1)
                elif k == "PJ":
                    i = s[1]
                    dve.wait_ge(qk_hi_ready, T * b + i + 1)
                    v.tensor_copy(qk[:, i, 1, :, HD:2 * HD], qk[:, i, 1, :, 0:HD])
                    v.tensor_copy(qk[:, i, 0, :, 2 * HD:3 * HD], qk[:, i, 0, :, 0:HD])
                    v.tensor_tensor(qk[:, i, 0, :, HD:2 * HD], bank[:, 0:P].rearrange("p (h e) -> p h e", e=HD),
                                    qk[:, i, 0, :, 0:HD], ALU.subtract)
                    v.tensor_tensor(qk[:, i, 1, :, 2 * HD:3 * HD], bank[:, P:2 * P].rearrange("p (h e) -> p h e", e=HD),
                                    qk[:, i, 1, :, 0:HD], ALU.subtract).then_inc(qk_lo_ready, 1)
                elif k == "VS":
                    dve.wait_ge(v1_ready, b + 1)
                    v.tensor_tensor(vr[:, :, :, :], vr[:, :, :, :], v_op[:, :, :, 0:HD], ALU.subtract).then_inc(v_rest_ready, 1)
                    dve.wait_ge(v_rest_ready, b + 1)
                    v.tensor_copy(v_op[:, :, :, HD:2 * HD], vr[:, :, :, :]).then_inc(v2_ready, 1)
                elif k == "MX":
                    g, u = s[1], s[2]
                    pair, w, head = unit(g, u)
                    h = HG * g + head
                    ring_full(dve, p, s, c)
                    blocks = bank[:, :].rearrange("p (k s) -> p k s", k=4)
                    if w in (0, 2):
                        dst = bmax[:, h, 0:4]
                    elif w in (1, 3):
                        dst = bmax[:, h, 4:8]
                    else:
                        dst = bmax[:, HG * g + 2 * pair:HG * g + 2 * pair + 2, 8:10]
                        blocks = bank[:, :].rearrange("p (h k s) -> p h k s", h=2, k=2)
                    v.tensor_reduce(dst, blocks, X, ALU.max).then_inc(bmax_ready, 1)
                elif k == "NM":
                    g = s[1]
                    dve.wait_ge(bmax_ready, 40 * b + UNITS * g + UNITS)
                    dve.wait_ge(m_cleared, b + 1)
                    hs = slice(HG * g, HG * g + HG)
                    for i, (lo, hi) in enumerate(((7, 8), (8, 10), (4, 7), (0, 4))):
                        last = v.tensor_reduce(nmax[:, i, :], bmax[:, hs, lo:hi], X, ALU.max, negate=True)
                    last.then_inc(nmax_ready, 1)
                    dve.wait_ge(nmax_ready, HG * b + g + 1)
                    v.tensor_copy(qk[:, :, 0, hs, 3 * HD].bitcast(F32R), nmax[:, :, :]).then_inc(m_hi_ready, 1)
                    dve.wait_ge(m_hi_ready, HG * b + g + 1)
                    v.tensor_tensor(qk[:, :, 0, hs, 3 * HD + 1], nmax[:, :, :], qk[:, :, 0, hs, 3 * HD],
                                    ALU.subtract).then_inc(m_ready, 1)
                elif k == "PH":
                    h = s[1]
                    dve.wait_ge(p_masked, HEADS * b + h + 1)
                    since(dve, pv_done, HEADS * b + h - 3)
                    v.tensor_copy(p_hi[:, h % 4, :], p32[:, h % 4, :]).then_inc(p_hi_ready, 1)
                elif k == "ON":
                    g = s[1]
                    dve.wait_ge(pv_done, HEADS * b + HG * g + HG)
                    o = pv_ps[:, :].rearrange("p (n c) -> p n c", c=VW)
                    v.tensor_reduce(osum[:, :, :], o[:, :, 0:3 * HD].rearrange("p n (k e) -> p n e k", k=3), X, ALU.add)
                    v.reciprocal(rden[:, :], o[:, :, 3 * HD]).then_inc(pv_read, 1)
                    dve.wait_ge(pv_read, HG * b + g + 1)
                    for i in range(T):
                        r = rden[:, HG * i:HG * i + HG].rearrange("p (h a) -> p h a", a=1).broadcast_to([P, HG, HD])
                        last = v.tensor_tensor(attn[:, i, HG * g:HG * g + HG, :], osum[:, HG * i:HG * i + HG, :], r, ALU.mult)
                    last.then_inc(attn_ready, 1)
                    dve.wait_ge(attn_ready, HG * b + g + 1)
                elif k == "WO":
                    ring_full(dve, p, s, c)
                    if isinstance(b, int):
                        dve.wait_ge(w_lo_ready, 2 * E)
                    dve.wait_ge(xr_ready, b + 1)
                    since(dve, acc_begun, b)
                    v.tensor_tensor(x1[:, :, :], bank[:, :].rearrange("p (t d) -> p t d", t=T), xr[:, :, :],
                                    ALU.add).then_inc(x1_ready, 1)
                    dve.wait_ge(x1_ready, b + 1)
                    norm_stats(x1, stats2, mv2, stats2_ready, 2 * b)
                elif k == "X2N":
                    dve.wait_ge(rs2_step, 2 * b + 2)
                    dve.wait_ge(y_t_ready, after_next(b))
                    for i in range(T):
                        last = v.tensor_scalar(xn2[:, i, :], x1[:, i, :], mv2[:, i, 0:1], rs2[:, 1, i:i + 1], ALU.subtract, ALU.mult)
                    last.then_inc(xn2_ready, 1)
                elif k == "GT":
                    z = 8 * b
                    ring_full(dve, p, s, c)
                    v.tensor_copy(gate[:, :, :], bank[:, 0:T * E].rearrange("p (t e) -> p t e", t=T)).then_inc(gate_step, 1)
                    dve.wait_ge(gate_step, z + 1)
                    apart(dve)
                    for i in range(T):
                        last = v.max(top[:, i, :], gate[:, i, :])
                    last.then_inc(gate_step, 1)
                    dve.wait_ge(gate_step, z + 2)
                    v.tensor_tensor(gsel[:, :, :], gate[:, :, :], top[:, :, 1:2].broadcast_to([P, T, E]), ALU.is_ge)
                    v.tensor_tensor(gate[:, :, :], gate[:, :, :], top[:, :, 0:1].broadcast_to([P, T, E]), ALU.subtract).then_inc(gate_step, 1)
                elif k == "GE":
                    z = 8 * b
                    dve.wait_ge(gexp_ready, b + 1)
                    v.tensor_tensor(gsel[:, :, :], gexp[:, :, :], gsel[:, :, :], ALU.mult).then_inc(gate_step, 1)
                    dve.wait_ge(gate_step, z + 4)
                    v.tensor_reduce(gsum[:, :], gsel[:, :, :], X, ALU.add).then_inc(gate_step, 1)
                    dve.wait_ge(gate_step, z + 5)
                    v.reciprocal(gsum[:, :], gsum[:, :]).then_inc(gate_step, 1)
                    dve.wait_ge(gate_step, z + 6)
                    v.tensor_tensor(gate[:, :, :], gsel[:, :, :], gsum[:, :].rearrange("p (t a) -> p t a", a=1).broadcast_to([P, T, E]),
                                    ALU.mult).then_inc(gate_step, 1)
                    dve.wait_ge(gate_step, z + 7)
                    if isinstance(b, int):
                        dve.wait_ge(m_tok_cleared, 1)
                    v.tensor_scalar(m_tok[:, :, 0:E].bitcast(F32R), gate[:, :, :], 1.0 / E, None, ALU.mult)
                    v.tensor_scalar(m_tok[:, :, 64:64 + E].bitcast(F32R), gate[:, :, :], 1.0 / E, None, ALU.mult).then_inc(gate_step, 1)
                    dve.wait_ge(gate_step, z + 8)
                    v.scalar_tensor_tensor(out=m_tok[:, :, 32:32 + E], in0=gate[:, :, :], scalar=1.0 / E, in1=m_tok[:, :, 0:E],
                                           op0=ALU.mult, op1=ALU.subtract).then_inc(m_tok_ready, 1)
                elif k == "XE":
                    e = s[1]
                    dve.wait_ge(l1_filled, L1_USES * f + L1_AT[s] + 1)
                    dve.wait_ge(x2_t_ready, f + 1)
                    since(dve, xe_lo_ready, E * f + max(e - 1, 0))
                    v.scalar_tensor_tensor(out=xe[:, e % 2, :], in0=x2_t[:, :], scalar=1.0, in1=l1_ps[:, L1_AT[s] % 2, :],
                                           op0=ALU.add, op1=ALU.mult).then_inc(xe_ready, 1)
                elif k == "WB":
                    dve.wait_ge(b2_hi_ready, 1)
                    v.tensor_tensor(b2_x[64:64 + R, :], b2_f[64:64 + R, :], b2_x[64:64 + R, :].bitcast(F32), ALU.subtract).then_inc(b2_hi_ready, 1)
                elif k == "W" and s[1] < E:
                    e = s[1]
                    dve.wait_ge(w1_mean, e + 1)
                    if e >= 2:
                        dve.wait_ge(w_lo_ready, e - 1)
                    else:
                        dve.wait_ge(pick_ready, 1)
                    v.tensor_tensor(w1c[:, e % 2, :], stage[e % STAGES], l1_ps[:, e % 2, :], ALU.subtract).then_inc(w1_centred, 1)
                elif k == "L1":
                    n = s[1]
                    dve.wait_ge(h_hi_ready, N1 * f + n + 1)
                    since(dve, l2_done, N1 * f + max(n - 2, 0))
                    v.scalar_tensor_tensor(out=h_lo[:, n % 3, :], in0=l1_ps[:, L1_AT[s] % 2, :], scalar=0.0,
                                           in1=h_hi[:, n % 3, :].bitcast(F32), op0=ALU.max, op1=ALU.subtract).then_inc(h_lo_ready, 1)
                elif k == "OT":
                    dve.wait_ge(ot_filled, f + 1)
                    since(dve, out_stored, 16 * f)
                    v.tensor_copy(ob[:, :, :], pv_ps[:, :].rearrange("p (t d) -> p t d", t=T)).then_inc(ob_ready, 1)

            all_passes(dve, "vector", one)

        @block.tensor
        def _(pe):
            t = nc.tensor

            def turn(bank, src):
                for i in range(T):
                    last = t.transpose(bank[:, i * P:(i + 1) * P], src(i), ident[:, :])
                return last

            def one(p, s, c, b, f):
                k = s[0]
                if k in RING_STEPS:
                    ring_free(pe, p, s, c)
                    bank = ring_bank(p, s)
                elif s in L1_AT:
                    l1_free(pe, s, f)
                    bank = l1_ps[:, L1_AT[s] % 2, :]
                if k == "YT":
                    if isinstance(b, int):
                        pe.wait_ge(consts_built, 1)
                    pe.wait_ge(yn_ready, b + 1)
                    turn(bank, lambda i: yn[:, i, :]).then_inc(ring_filled, 1)
                elif k == "PJ":
                    i = s[1]
                    pe.wait_ge(y_t_ready, b + 1)
                    if isinstance(b, int) and b == 0:
                        pe.wait_ge(wqkv_loaded, 16)
                    t.matmul(bank[:, 0:3 * P], y_t[:, i * P:(i + 1) * P], wqkv_s[:, :], start=True, stop=True).then_inc(ring_filled, 1)
                elif k in ("KT", "QT"):
                    g = s[1]
                    pe.wait_ge(qk_lo_ready, T * b + T)
                    if k == "QT":
                        pe.wait_ge(m_cleared, b + 1)
                    which = 1 if k == "KT" else 0
                    turn(bank, lambda i: qk[:, i, which, HG * g:HG * g + HG, :].rearrange("p h r -> p (h r)")).then_inc(ring_filled, 1)
                elif k == "QM":
                    g = s[1]
                    pe.wait_ge(m_ready, HG * b + g + 1)
                    turn(bank, lambda i: qk[:, i, 0, HG * g:HG * g + HG, :].rearrange("p h r -> p (h r)")).then_inc(ring_filled, 1)
                elif k == "MX":
                    g, u = s[1], s[2]
                    pair, v, head = unit(g, u)
                    pe.wait_ge(kz_ready, HEADS * b + HG * g + HG)
                    pe.wait_ge(q1_ready, HG * b + g + 1)

                    def rows(i, head, at):
                        n = (i + 1) * P
                        t.matmul(bank[:, at:at + n], q1[:, g % 2, i * P:(i + 1) * P], kz[:, g % 2, head, 0:n], start=True, stop=False)
                        return t.matmul(bank[:, at + n - P:at + n], ident_b[:, :], causal[:, :], start=False, stop=True)

                    if v in (0, 2):
                        last = rows(3, head, 0)
                    elif v in (1, 3):
                        rows(2, head, 0)
                        last = rows(0, head, 3 * P)
                    else:
                        rows(1, 2 * pair, 0)
                        last = rows(1, 2 * pair + 1, 2 * P)
                    last.then_inc(ring_filled, 1)
                elif k == "ST":
                    g, u = s[1], s[2]
                    pair, v, head = unit(g, u)
                    n = 10 * g + u
                    since(pe, exp_ready, 40 * b + n - 1)
                    pe.wait_ge(q2_ready, HG * b + g + 1)
                    st = st_ps[:, n % 2, :]

                    def cols(j, head, lo, hi, at):
                        return t.matmul(st[:, at:at + (hi - lo) * P], kz[:, g % 2, head, j * P:(j + 1) * P],
                                        q2[:, g % 2, lo * P:hi * P], start=True, stop=True)

                    if v in (0, 2):
                        for j in range(T):
                            last = cols(j, head, j, j + 1, j * P)
                    elif v in (1, 3):
                        cols(0, head, 1, 4, 0)
                        last = cols(2, head, 3, 4, 3 * P)
                    else:
                        cols(1, 2 * pair, 2, 4, 0)
                        last = cols(1, 2 * pair + 1, 2, 4, 2 * P)
                    last.then_inc(st_filled, 1)
                elif k == "PV":
                    h = s[1]
                    pe.wait_ge(p_lo_ready, HEADS * b + h + 1)
                    if h == 0:
                        pe.wait_ge(v3_ready, b + 1)
                        since(pe, ob_ready, b - 1)
                    if h % HG == 0:
                        since(pe, pv_read, HG * b + h // HG)
                    at = {(j, j): j for j in range(T)}
                    at.update({(0, 1): 4, (0, 2): 5, (0, 3): 6, (2, 3): 7, (1, 2): 8, (1, 3): 9})
                    for i in range(T):
                        o = pv_ps[:, (HG * i + h % HG) * VW:(HG * i + h % HG) * VW + 3 * HD + 1]
                        for j in range(i + 1):
                            col = at[(j, i)] * P
                            rhs = v_op[:, j, h, 0:3 * HD + 1]
                            t.matmul(o, p_hi[:, h % 4, col:col + P], rhs, start=(j == 0), stop=False)
                            last = t.matmul(o, p_lo[:, h % 4, col:col + P], rhs, start=False, stop=(j == i))
                    last.then_inc(pv_done, 1)
                elif k == "AT":
                    pe.wait_ge(attn_ready, HG * b + HG)
                    turn(bank, lambda i: attn[:, i, :, :].rearrange("p h e -> p (h e)")).then_inc(ring_filled, 1)
                elif k == "WO":
                    pe.wait_ge(a_t_ready, b + 1)
                    if isinstance(b, int) and b == 0:
                        pe.wait_ge(consts_loaded, 16 * CONSTS)
                    for i in range(T):
                        last = t.matmul(bank[:, i * P:(i + 1) * P], a_t[:, i * P:(i + 1) * P], wo_s[:, :], start=True, stop=True)
                    last.then_inc(ring_filled, 1)
                elif k == "X2T":
                    pe.wait_ge(xn2_ready, b + 1)
                    turn(bank, lambda i: xn2[:, i, :]).then_inc(ring_filled, 1)
                elif k == "GT":
                    pe.wait_ge(x2_t_ready, b + 1)
                    for i in range(T):
                        last = t.matmul(bank[:, i * E:(i + 1) * E], x2_t[:, i * P:(i + 1) * P], wg_s[:, :], start=True, stop=True)
                    last.then_inc(ring_filled, 1)
                elif k == "MKT":
                    pe.wait_ge(m_tok_ready, b + 1)
                    turn(bank, lambda i: m_tok[:, i, :]).then_inc(ring_filled, 1)
                elif k == "W" and s[1] < E:
                    e = s[1]
                    pe.wait_ge(stage_loaded[e % STAGES], 16 * (e // STAGES + 1))
                    pe.wait_ge(b1_scaled, 1)
                    if e >= 2:
                        pe.wait_ge(w1_centred, e - 1)
                    t.matmul(l1_ps[:, e % 2, :], mean_w, stage[e % STAGES], start=True, stop=False)
                    t.matmul(l1_ps[:, e % 2, :], pick[0:E, e, :].bitcast(F32), b1_s[:, :], start=False, stop=True).then_inc(w1_mean, 1)
                elif k == "XE":
                    e = s[1]
                    pe.wait_ge(m_t_ready, f + 1)
                    pe.wait_ge(w_lo_ready, 2 * E)
                    t.matmul(bank[:, :], pick[:, e, :], m_t[:, :], start=True, stop=True).then_inc(l1_filled, 1)
                elif k == "ACC0":
                    since(pe, acc_saved, f)
                    pe.wait_ge(m_t_ready, f + 1)
                    pe.wait_ge(x1_ready, f + 1)
                    pe.wait_ge(b2_hi_ready, 2)
                    t.matmul(acc_ps[:, :], b2_x[:, :], m_t[:, :], start=True, stop=False)
                    for i in range(T):
                        last = t.matmul(acc_ps[:, i * P:(i + 1) * P], x1[:, i, :], ident[:, :], start=False, stop=False)
                    last.then_inc(acc_begun, 1)
                elif k == "L1":
                    n = s[1]
                    e, chunk = n // C, n % C
                    if chunk == 0:
                        pe.wait_ge(xe_lo_ready, E * f + e + 1)
                    w = slice(chunk * P, chunk * P + P)
                    t.matmul(bank, w1_lo[:, e, w], xe_hi[:, e % 2, :], start=True, stop=False)
                    t.matmul(bank, w1_hi[:, e, w], xe_lo[:, e % 2, :], start=False, stop=False)
                    t.matmul(bank, w1_hi[:, e, w], xe_hi[:, e % 2, :], start=False, stop=True).then_inc(l1_filled, 1)
                elif k == "L2":
                    n = s[1]
                    pe.wait_ge(h_lo_ready, N1 * f + n + 1)
                    t.matmul(acc_ps[:, :], w2_lo[:, n, :], h_hi[:, n % 3, :], start=False, stop=False)
                    t.matmul(acc_ps[:, :], w2_hi[:, n, :], h_lo[:, n % 3, :], start=False, stop=False)
                    t.matmul(acc_ps[:, :], w2_hi[:, n, :], h_hi[:, n % 3, :], start=False, stop=(n == N1 - 1)).then_inc(l2_done, 1)
                elif k == "OT":
                    pe.wait_ge(acc_saved, f + 1)
                    pe.wait_ge(pv_read, HG * (min(c + 1, B) if isinstance(c, int) else c + 1))
                    since(pe, ob_ready, f)
                    turn(pv_ps, lambda i: acc_s[:, i * P:(i + 1) * P]).then_inc(ot_filled, 1)

            all_passes(pe, "tensor", one)


_INS = ["x", "ln_w", "ln_b", "wqkv", "wo", "w_gate", "w1", "b1", "w2", "b2"]


def kernel(L0_attn_x, L0_attn_ln_w, L0_attn_ln_b, L0_attn_wq, L0_attn_wk, L0_attn_wv, L0_attn_wo,
           L0_ffn_W_gate, L0_ffn_W1, L0_ffn_b1, L0_ffn_W2, L0_ffn_b2):
    import numpy as _np
    import concourse.bacc as _bacc
    from concourse import mybir as _mybir
    from concourse.bass_utils import run_bass_kernel_spmd as _run

    def by_input(w):
        return _np.transpose(_np.asarray(w), (1, 0, 2)).reshape(w.shape[1], -1)

    wqkv = _np.concatenate([by_input(w) for w in (L0_attn_wq, L0_attn_wk, L0_attn_wv)], axis=1)
    given = [L0_attn_x, L0_attn_ln_w, L0_attn_ln_b, wqkv, L0_attn_wo, L0_ffn_W_gate, L0_ffn_W1, L0_ffn_b1, L0_ffn_W2, L0_ffn_b2]
    nc = _bacc.Bacc("TRN2", target_bir_lowering=False, num_devices=1)
    arrays, args = {}, []
    for name, a in zip(_INS, given):
        a = _np.ascontiguousarray(a)
        arrays[f"in_{name}_dram"] = a
        args.append(nc.dram_tensor(f"in_{name}_dram", a.shape, _mybir.dt.from_np(a.dtype), kind="ExternalInput").ap())
    out = nc.dram_tensor("out_dram", arrays["in_x_dram"].shape, _mybir.dt.float32, kind="ExternalOutput").ap()
    moe_block_kernel(nc, *args, out)
    r = _run(nc, [arrays], core_ids=[0])
    return r.results[0]["out_dram"]
```

```python
from contextlib import ExitStack

import concourse.bass as bass
from concourse import mybir

P = 128
F32 = mybir.dt.float32
F32R = mybir.dt.float32r
F16 = mybir.dt.float16
BF16 = mybir.dt.bfloat16
ALU = mybir.AluOpType
ACT = mybir.ActivationFunctionType
X = mybir.AxisListType.X
EPS = 1e-5
MASKED = -1e30
UNITS = 10


AHEAD_W = 2

TIMES = {
    "WB": 37.31, "W0": 42.09, "pace": 0.94, "pace'": 1.62, "PV end": 0.3, "X1K": 10.86, "KT": -2.24,
    "QT": -3.68, "QM": -2.23, "NM": -0.86, "ST": 0.18, "PM0": -0.77, "PM1": -0.31, "PH0": 1.32, "PH1": 3.15,
    "LO0": 1.33, "LO1": 1.39, "PV0": 6.4, "PV1": 6.99, "ON": 1.46, "LN1": 31.15, "YN": 35.85, "YT": 35.03,
    "PJ": 37.93, "PJ_step": 0.85, "QC": 36.93, "KT'": 41.41, "QT'": 43.56, "MX'": 47.07, "NM'": 18.77,
    "AT": -0.4, "WO": -0.21, "X2N": 3.0, "X2T": 5.6, "VS": 7.81, "GT": 6.68, "GE": 7.35, "XN": 9.12,
    "MKT": 10.68, "L2": 2.92, "XE": -5.79, "ACC0": 2.7, "W": 1.91, "OA": -0.11, "OT": 2.73, "LENGTH": 68.15,
}
GROUPS = [1.03, 13.75, 26.48, 39.24]
EXPERTS = [4.89, 10.52, 19.93, 27.38, 31.59, 40.96, 46.5, 56.56, 65.31]
LATE = {
    "scalar": {
        "ST": -0.34, "PJ": -0.04, "YT": 0.43, "QM": 0.03, "KT": -0.27, "XE": 0.33, "QT": -0.72, "L1": -0.49, "X1K": -0.91, "AT": 0.06, "MKT": 5.57, "VS": -3.02, "X2T": -0.38},
    "vector": {
        "L1": 0.59, "XE": -0.02, "YN": -5.53, "LN1": -2.98, "MX": -0.02, "PJ": -0.08, "NM": 1.77, "ON": -1.6, "X2N": 0.82, "VS": 2.0, "OT": 2.83, "WO": 1.13, "XN": 1.2, "GT": -0.67, "GE": 1.54},
    "gpsimd": {"XE": -0.03, "LN1": -1.9, "QC": -2.55, "VS": -6.69, "XN": -4.73, "WO": 1.3},
    "tensor": {},
}


def schedule(batch=True, ahead=True, beside=None, late=True):
    t, steps = TIMES, []

    def add(time, *step):
        if batch:
            steps.append((time, step))

    def add_next(time, *step):
        if ahead:
            steps.append((time, step + ("next",)))

    def unit_time(n):
        return GROUPS[n // UNITS] + t["pace"] * (n % UNITS)

    for g in range(4):
        begin = unit_time(UNITS * g)
        if g < 3:
            add(begin + t["KT"], "KT", g + 1)
            add(begin + t["QT"], "QT", g + 1)
        add(begin + t["QM"], "QM", g)
        for u in range(UNITS):
            if g < 3:
                add(unit_time(UNITS * g + u), "MX", g + 1, u)
            add(unit_time(UNITS * g + u) + t["ST"], "ST", g, u)
        if g < 3:
            add(unit_time(UNITS * g + UNITS - 1) + t["NM"], "NM", g + 1)
    for h in range(16):
        ready, second = unit_time(5 * (h // 2) + 4), str(h % 2)
        for k in ("PM", "PH", "LO"):
            add(ready + t[k + second], k, h)
        pv = ready + t["PV" + second] + t["PV end"] * max(h - 12, 0)
        add(pv, "PV", h)
        if h % 4 == 3:
            add(pv + t["ON"], "ON", h // 4)
    done = pv + t["ON"]
    for k in ("AT", "WO", "X2N", "X2T", "GT", "GE", "MKT"):
        add(done + t[k], k)
    for k in ("VS", "XN"):
        add_next(done + t[k], k)
    for k in ("LN1", "YN", "YT", "QC"):
        add_next(t[k], k)
    for i in range(4):
        add_next(t["PJ"] + i * t["PJ_step"], "PJ", i)
    add_next(t["KT'"], "KT", 0)
    add_next(t["QT'"], "QT", 0)
    for u in range(UNITS):
        add_next(t["MX'"] + t["pace'"] * u, "MX", 0, u)
    add_next(t["MX'"] + t["pace'"] * (UNITS - 1) + t["NM'"], "NM", 0)
    if beside == "tables":
        steps.append((t["WB"], ("WB",)))
    if beside in ("tables", "weights"):
        for n in range(AHEAD_W) if beside == "tables" else range(AHEAD_W, 16):
            steps.append((t["W0"] + t["W"] * n if n < AHEAD_W else t["W"] * (n - AHEAD_W), ("W", n)))
    ffn = [(t["X1K"], ("X1K",)), (t["ACC0"], ("ACC0",))]
    for n in range(32):
        e = n // 4
        time = EXPERTS[e] + (n % 4) * (EXPERTS[e + 1] - EXPERTS[e]) / 4
        if n % 4 == 0:
            ffn.append((time + t["XE"], ("XE", n // 4)))
        ffn.append((time, ("L1", n)))
        ffn.append((time + t["L2"], ("L2", n)))
    ffn.append((time + t["L2"] + t["OA"], ("OA",)))
    ffn.append((time + t["L2"] + t["OT"], ("OT",)))
    if beside == "ffn":
        steps += [(time, s) for time, s in ffn if time < t["LENGTH"]]
    if beside == "ffn" and late or beside == "late":
        steps += [(time - t["LENGTH"], s + ("late",)) for time, s in ffn if time >= t["LENGTH"]]
    return steps


def order(steps, engine):
    late = LATE[engine]
    result = [s for _, s in sorted(steps, key=lambda x: x[0] + late.get(x[1][0], 0.0))]
    for kind in {s[0] for s in result}:
        same = [s for s in result if s[0] == kind]
        assert same == sorted(same, key=lambda s: ({"late": 0, "next": 2}.get(s[-1], 1), s))
    return result


def buffers_kept(steps):
    at = {s: n for n, s in enumerate(order(steps, "tensor"))}

    def first_then(one, other):
        assert one not in at or other not in at or at[one] < at[other]

    first_then(("QM", 3), ("PJ", 0, "next"))
    first_then(("PJ", 3, "next"), ("AT",))
    for g in range(2, 5):
        kt, qt = (("KT", g), ("QT", g)) if g < 4 else (("KT", 0, "next"), ("QT", 0, "next"))
        first_then(("ST", g - 2, UNITS - 1), kt)
        first_then(("MX", g - 2, UNITS - 1), kt)
        first_then(("MX", g - 2, UNITS - 1), qt)
        if g < 4:
            first_then(("ST", g - 2, UNITS - 1), ("QM", g))
    for e in range(2, 8):
        first_then(("L1", 4 * e - 5), ("XE", e))
    first_then(("ACC0",), ("L2", 0))
    first_then(("L2", 31, "late"), ("ACC0",))
    first_then(("OT", "late"), ("PV", 0))
    first_then(("PV", 15), ("OT",))
    assert not any(s[0] == "XE" and s[-1] == "late" for s in at)


AHEAD = schedule(batch=False, beside="tables")
FIRST = schedule(beside="weights")
SECOND = schedule(beside="ffn", late=False)
STEPS = schedule(beside="ffn")
LAST = schedule(ahead=False, beside="ffn")
FFN_LAST = schedule(batch=False, ahead=False, beside="ffn")
FFN_REST = schedule(batch=False, ahead=False, beside="late")
for steps in (AHEAD, FIRST, SECOND, STEPS, LAST, FFN_LAST, FFN_REST):
    buffers_kept(steps)

RING_STEPS = ("YT", "PJ", "KT", "QT", "MX", "QM", "AT", "WO", "X2T", "GT", "MKT")


def ring_users(steps):
    return [s for s in order(steps, "tensor") if s[0] in RING_STEPS]


RING = len(ring_users(STEPS))
RING_AHEAD = len(ring_users(AHEAD))
FFN_ORDER = [s for s in order(SECOND, "tensor") if s[0] in ("XE", "L1", "L2")] + \
    [s[:-1] for s in order(FFN_REST, "tensor") if s[0] in ("XE", "L1", "L2")]
L1_AT = {s: n for n, s in enumerate([s for s in FFN_ORDER if s[0] in ("XE", "L1")])}
L1_USES = len(L1_AT)
assert RING % 2 == 0 and L1_USES % 2 == 0


class Pass:

    def __init__(self, steps, before, start):
        self.steps = {engine: order(steps, engine) for engine in LATE}
        self.start = start
        self.users = (ring_users(before) if before else [None, None])[-2:] + ring_users(steps)
        self.at = {s: n for n, s in enumerate(ring_users(steps))}


def moe_block_kernel(nc, x, ln_w, ln_b, wqkv, wo, w_gate, w1, b1, w2, b2, out):
    B, S, D = x.shape
    E, _, H = w1.shape
    T = S // P
    HEADS, HD = 16, 8
    HG = 4
    R = 32
    C = H // P
    N1 = E * C
    BLK = 10
    SCALE = float(HD) ** -0.5
    VW = 32

    x_t = x.rearrange("b (t p) d -> b p t d", p=P)
    out_t = out.rearrange("b (t p) d -> b p t d", p=P)
    w1_t = w1.rearrange("e d h -> d e h")
    w2_t = w2.rearrange("e (c p) d -> p e c d", p=P)

    with ExitStack() as ctx:
        def sb(name, shape, dt=F32):
            return ctx.enter_context(nc.sbuf_tensor(name, shape, dt))

        def sem(name):
            return ctx.enter_context(nc.semaphore(name))

        ring = ctx.enter_context(nc.psum_tensor("ring", [P, 2, 512], F32))
        st_ps = ctx.enter_context(nc.psum_tensor("st_ps", [P, 2, 512], F32))
        l1_ps = ctx.enter_context(nc.psum_tensor("l1_ps", [P, 2, 512], F32))
        acc_ps = ctx.enter_context(nc.psum_tensor("acc_ps", [P, 512], F32))
        pv_ps = ctx.enter_context(nc.psum_tensor("pv_ps", [P, 512], F32))

        ident = sb("ident", [P, P])
        ident_b = sb("ident_b", [P, P], BF16)
        causal = sb("causal", [P, P], BF16)
        pick = sb("pick", [P, E], F32R)
        half_neg = sb("half_neg", [P, T])
        eps = sb("eps", [P, T])
        lnw = sb("lnw", [P, 1])
        lnb = sb("lnb", [P, 1])
        wqkv_s = sb("wqkv_s", [P, 3 * P])
        wo_s = sb("wo_s", [P, D])
        wg_s = sb("wg_s", [P, E])
        b1_s = sb("b1_s", [E, H])
        b2_x = sb("b2_x", [P, D], F32R)
        w1_hi = sb("w1_hi", [P, E, H], F32R)
        w1_lo = sb("w1_lo", [P, E, H], F32R)
        w2_hi = sb("w2_hi", [P, N1, D], F32R)
        w2_lo = sb("w2_lo", [P, N1, D], F32R)
        xb = sb("xb", [P, T, D])
        stats = sb("stats", [P, T, 6])
        mv = sb("mv", [P, T, 2])
        rs = sb("rs", [P, 6, T])
        stats2 = sb("stats2", [P, T, 6])
        mv2 = sb("mv2", [P, T, 2])
        rs2 = sb("rs2", [P, 2, T])
        yn = sb("yn", [P, T, D])
        xn = sb("xn", [P, T, D])
        xr = xn
        y_t = sb("y_t", [P, S])
        qk = sb("qk", [P, T, 2, HEADS, R])
        vr = sb("vr", [P, T, HEADS, HD])
        v_op = sb("v_op", [P, T, HEADS, VW], BF16)
        kz = sb("kz", [P, 2, HG, S], F32R)
        q1 = sb("q1", [P, 2, S], F32R)
        q2 = sb("q2", [P, 2, S], F32R)
        bmax = sb("bmax", [P, HEADS, BLK])
        nmax = sb("nmax", [P, T, HG])
        p32 = sb("p32", [P, 4, BLK * P])
        p_hi = sb("p_hi", [P, 4, BLK * P], F16)
        p_lo = sb("p_lo", [P, 4, BLK * P], F16)
        osum = sb("osum", [P, T * HG, HD])
        rden = sb("rden", [P, T * HG])
        attn = sb("attn", [P, T, HEADS, HD])
        a_t = y_t
        x1 = sb("x1", [P, T, D])
        x1_keep = sb("x1_keep", [P, T, D])
        xn2 = yn
        x2_t = sb("x2_t", [P, S])
        gate = sb("gate", [P, T, E])
        top = sb("top", [P, T, 8])
        gsel = sb("gsel", [P, T, E])
        gexp = sb("gexp", [P, T, E])
        gsum = sb("gsum", [P, T])
        m_tok = sb("m_tok", [P, T, P])
        m_t = sb("m_t", [P, S], F32R)
        xe = sb("xe", [P, 2, S])
        xe_hi = sb("xe_hi", [P, 2, S], F32R)
        xe_lo = sb("xe_lo", [P, 2, S], F32R)
        h_hi = sb("h_hi", [P, 3, S], F32R)
        h_lo = sb("h_lo", [P, 3, S], F32R)
        acc_s = sb("acc_s", [P, S])
        ob = sb("ob", [P, T, D])
        stage = [acc_s[:, :], ob[:, :, :].rearrange("p t d -> p (t d)"), x2_t[:, :], x1[:, :, :].rearrange("p t d -> p (t d)")]
        STAGES = len(stage)
        pick_f = m_tok[:, 2, 0:E]
        w1c = xe
        mean_w = m_tok[:, 0, :]
        b2_f = m_tok[:, 1, :]

        consts_loaded = sem("consts_loaded")
        stage_loaded = [sem(f"stage_loaded{k}") for k in range(STAGES)]
        x_loaded = sem("x_loaded")
        out_stored = sem("out_stored")
        waited_apart = sem("waited_apart")
        tables_set = sem("tables_set")
        qk_cleared = sem("qk_cleared")
        kz_cleared = sem("kz_cleared")
        picks_set = sem("picks_set")
        m_tok_cleared = sem("m_tok_cleared")
        b2_f_cleared = sem("b2_f_cleared")
        norm_loaded = sem("norm_loaded")
        wqkv_loaded = sem("wqkv_loaded")
        consts_built = sem("consts_built")
        b1_scaled = sem("b1_scaled")
        w1_mean = sem("w1_mean")
        w1_centred = sem("w1_centred")
        w_hi_ready = sem("w_hi_ready")
        w1_lo_ready = sem("w1_lo_ready")
        w2_lo_ready = sem("w2_lo_ready")
        b2_hi_ready = sem("b2_hi_ready")
        pick_ready = sem("pick_ready")
        stats_ready = sem("stats_ready")
        rs_step = sem("rs_step")
        stats2_ready = sem("stats2_ready")
        rs2_step = sem("rs2_step")
        yn_ready = sem("yn_ready")
        v_raw_ready = sem("v_raw_ready")
        rstd_ready = sem("rstd_ready")
        xn_ready = sem("xn_ready")
        xr_ready = sem("xr_ready")
        ring_filled = sem("ring_filled")
        y_t_ready = sem("y_t_ready")
        qk_hi_ready = sem("qk_hi_ready")
        qk_lo_ready = sem("qk_lo_ready")
        v1_ready = sem("v1_ready")
        v_rest_ready = sem("v_rest_ready")
        v2_ready = sem("v2_ready")
        v3_ready = sem("v3_ready")
        kz_ready = sem("kz_ready")
        q1_ready = sem("q1_ready")
        q2_ready = sem("q2_ready")
        bmax_ready = sem("bmax_ready")
        nmax_ready = sem("nmax_ready")
        m_cleared = sem("m_cleared")
        m_hi_ready = sem("m_hi_ready")
        m_ready = sem("m_ready")
        st_filled = sem("st_filled")
        exp_ready = sem("exp_ready")
        p_masked = sem("p_masked")
        p_hi_ready = sem("p_hi_ready")
        p_lo_ready = sem("p_lo_ready")
        pv_done = sem("pv_done")
        pv_read = sem("pv_read")
        attn_ready = sem("attn_ready")
        a_t_ready = sem("a_t_ready")
        x1_ready = sem("x1_ready")
        xn2_ready = sem("xn2_ready")
        x2_t_ready = sem("x2_t_ready")
        gate_step = sem("gate_step")
        gexp_ready = sem("gexp_ready")
        m_tok_ready = sem("m_tok_ready")
        m_t_ready = sem("m_t_ready")
        xe_ready = sem("xe_ready")
        xe_hi_ready = sem("xe_hi_ready")
        xe_lo_ready = sem("xe_lo_ready")
        x1_kept = sem("x1_kept")
        l1_filled = sem("l1_filled")
        h_hi_ready = sem("h_hi_ready")
        h_lo_ready = sem("h_lo_ready")
        l2_done = sem("l2_done")
        acc_saved = sem("acc_saved")
        ot_filled = sem("ot_filled")
        ob_ready = sem("ob_ready")

        def batch_of(step, b):
            return b + 1 if step[-1] == "next" else b

        def after_next(b):
            return min(b + 2, B) if isinstance(b, int) else b + 2

        CONSTS = 6

        def since(eng, signal, value):
            if not (isinstance(value, int) and value <= 0):
                eng.wait_ge(signal, value)

        def read_by(step, b):
            k, g = step[0], (step[1] if len(step) > 1 else 0)
            b = batch_of(step, b)
            return {
                "YT": lambda: (y_t_ready, b + 1),
                "PJ": lambda: (qk_lo_ready, T * b + g + 1),
                "KT": lambda: (kz_ready, HEADS * b + HG * g + HG),
                "QT": lambda: (q1_ready, HG * b + g + 1),
                "QM": lambda: (q2_ready, HG * b + g + 1),
                "MX": lambda: (bmax_ready, 40 * b + UNITS * g + step[2] + 1),
                "AT": lambda: (a_t_ready, b + 1),
                "WO": lambda: (x1_ready, b + 1),
                "X2T": lambda: (x2_t_ready, b + 1),
                "GT": lambda: (gate_step, 8 * b + 1),
                "MKT": lambda: (m_t_ready, b + 1),
                "XE": lambda: (xe_ready, E * b + g + 1),
                "L1": lambda: (h_lo_ready, N1 * b + g + 1),
            }[k]()

        def apart(eng):
            eng.sem_inc(waited_apart, 1)

        def ring_bank(p, step):
            return ring[:, (p.start + p.at[step]) % 2, :]

        def ring_free(eng, p, step, b):
            n = p.at[step]
            if p.users[n] is not None:
                eng.wait_ge(*read_by(p.users[n], b - 1 if n < 2 else b))

        def ring_full(eng, p, step, b):
            eng.wait_ge(ring_filled, RING * b + p.start + p.at[step] + 1)

        def l1_free(eng, step, f):
            users = list(L1_AT)
            n = L1_AT[step] - 2
            if n >= 0 and users[n][0] == "L1" and FFN_ORDER.index(("L2", users[n][1])) < FFN_ORDER.index(step):
                pass
            elif n >= 0:
                eng.wait_ge(*read_by(users[n], f))
            else:
                signal, value = read_by(users[n], f - 1)
                since(eng, signal, value)

        def unit(g, u):
            pair, v = u // 5, u % 5
            head = 2 * pair + (1 if v in (2, 3) else 0)
            return pair, v, head

        before_first = Pass(AHEAD, None, RING)
        first = Pass(FIRST, AHEAD, RING_AHEAD)
        second = Pass(SECOND, FIRST, RING_AHEAD)
        third = Pass(STEPS, SECOND, RING_AHEAD)
        middle = Pass(STEPS, STEPS, RING_AHEAD)
        last = Pass(LAST, STEPS, RING_AHEAD)
        ffn_last = Pass(FFN_LAST, None, 0)
        ffn_rest = Pass(FFN_REST, None, 0)

        def all_passes(eng, name, one):

            def run(p, b):
                for s in p.steps[name]:
                    if s[-1] == "late":
                        one(p, s[:-1], b, None, b - 2, True)
                    else:
                        one(p, s, b, batch_of(s, b), b - 1, False)

            run(before_first, -1)
            run(first, 0)
            run(second, 1)
            run(third, 2)
            with eng.Fori(3, B - 1) as b:
                run(middle, b)
            run(last, B - 1)
            run(ffn_last, B)
            run(ffn_rest, B + 1)

        block = ctx.enter_context(nc.Block())

        @block.sync
        def _(sp):
            sp.dma_start(xb[:, :, :], x_t[0]).then_inc(x_loaded, 16)
            sp.dma_start(lnw[:, :], ln_w.rearrange("(d a) -> d a", a=1)).then_inc(norm_loaded, 16)
            sp.dma_start(lnb[:, :], ln_b.rearrange("(d a) -> d a", a=1)).then_inc(norm_loaded, 16)
            sp.dma_start(wqkv_s[:, :], wqkv).then_inc(wqkv_loaded, 16)
            for dst, src in ((wo_s, wo), (wg_s, w_gate), (b1_s, b1)):
                sp.dma_start(dst[:, :], src).then_inc(consts_loaded, 16)
            sp.wait_ge(b2_f_cleared, 1)
            for k in range(3):
                sp.dma_start(b2_f[32 * k:32 * k + E, :], b2).then_inc(consts_loaded, 16)
            for n in range(2 * E):
                e = n % E
                if n >= STAGES:
                    sp.wait_ge(*((w1_lo_ready, n - STAGES + 1) if n < E + STAGES else (w2_lo_ready, n - STAGES - E + 1)))
                src = w1_t[:, e, :] if n < E else w2_t[:, e, :, :]
                dst = stage[n % STAGES] if n < E else stage[n % STAGES].rearrange("p (c d) -> p c d", c=C)
                sp.dma_start(dst, src).then_inc(stage_loaded[n % STAGES], 16)

            def load(b, src):
                sp.wait_ge(xr_ready, b + 1)
                sp.dma_start(xb[:, :, :], src).then_inc(x_loaded, 16)

            def store(f, dst):
                sp.wait_ge(ob_ready, f + 1)
                sp.dma_start(dst, ob[:, :, :]).then_inc(out_stored, 16)

            load(0, x_t[1])
            load(1, x_t[2])
            store(0, out_t[0])
            load(2, x_t[3])
            with sp.Fori(3, B - 1) as b:
                store(b - 2, out_t[bass.ds(b - 2, 1)].rearrange("a p t d -> p (a t) d"))
                load(b, x_t[bass.ds(b + 1, 1)].rearrange("a p t d -> p (a t) d"))
            store(B - 3, out_t[B - 3])
            store(B - 2, out_t[B - 2])
            store(B - 1, out_t[B - 1])
            sp.wait_ge(out_stored, 16 * B)

        @block.gpsimd
        def _(pool):
            g = nc.gpsimd
            g.memset(ident[:, :], 0.0)
            g.memset(causal[:, :], 0.0)
            g.memset(half_neg[:, :], -0.5)
            g.memset(eps[:, :], EPS).then_inc(tables_set, 1)
            g.memset(qk[:, :, :, :, :], 0.0)
            pool.wait_ge(tables_set, 1)
            g.affine_select(out=ident[:, :], in_=ident[:, :], compare_op=ALU.not_equal, fill=1.0, base=0,
                            pattern=[[-1, P]], channel_multiplier=1)
            g.affine_select(out=causal[:, :], in_=causal[:, :], compare_op=ALU.is_ge, fill=MASKED, base=0,
                            pattern=[[-1, P]], channel_multiplier=1).then_inc(tables_set, 1)
            pool.wait_ge(tables_set, 2)
            g.tensor_copy(ident_b[:, :], ident[:, :]).then_inc(consts_built, 1)
            g.memset(qk[:, :, 1, :, 3 * HD:3 * HD + 2], 1.0).then_inc(qk_cleared, 1)

            def power(dst, src, n):
                pool.wait_ge(rs_step, n)
                return g.tensor_tensor(dst, src, half_neg[:, :], ALU.pow)

            def one(p, s, c, b, f, late):
                k = s[0]
                if k == "LN1":
                    pool.wait_ge(stats_ready, 2 * b + 2)
                    z = 6 * b
                    g.tensor_tensor(rs[:, 0, :], mv[:, :, 1], eps[:, :], ALU.add).then_inc(rs_step, 1)
                    power(rs[:, 1, :], rs[:, 0, :], z + 1).then_inc(rs_step, 1)
                    pool.wait_ge(rs_step, z + 2)
                    g.tensor_tensor(rs[:, 2, :], rs[:, 1, :], mv[:, :, 1], ALU.mult).then_inc(rs_step, 1)
                    pool.wait_ge(rs_step, z + 3)
                    g.tensor_tensor(rs[:, 3, :], rs[:, 2, :], rs[:, 1, :], ALU.mult).then_inc(rs_step, 1)
                    pool.wait_ge(rs_step, z + 4)
                    g.tensor_tensor(rs[:, 4, :], rs[:, 3, :], eps[:, :], ALU.add).then_inc(rs_step, 1)
                    power(rs[:, 5, :], rs[:, 4, :], z + 5).then_inc(rs_step, 1)
                    pool.wait_ge(rs_step, z + 6)
                    g.tensor_tensor(rs[:, 0, :], rs[:, 5, :], rs[:, 1, :], ALU.mult).then_inc(rstd_ready, 1)
                elif k == "XN":
                    pool.wait_ge(xn_ready, b + 1)
                    g.tensor_tensor(xr[:, :, :], xb[:, :, :], xn[:, :, :], ALU.add).then_inc(xr_ready, 1)
                elif k == "QC":
                    if isinstance(b, int) and b == 0:
                        pool.wait_ge(qk_cleared, 1)
                    since(pool, q2_ready, HG * b)
                    apart(pool)
                    g.memset(qk[:, :, 0, :, 3 * HD:3 * HD + 2], 0.0).then_inc(m_cleared, 1)
                elif k == "VS":
                    pool.wait_ge(v2_ready, b + 1)
                    g.tensor_tensor(v_op[:, :, :, 2 * HD:3 * HD], vr[:, :, :, :], v_op[:, :, :, HD:2 * HD],
                                    ALU.subtract).then_inc(v3_ready, 1)
                elif k == "PM":
                    h = s[1]
                    pool.wait_ge(exp_ready, 40 * b + 10 * (h // 4) + 5 * (h % 4 // 2) + 5)
                    apart(pool)
                    v = p32[:, h % 4, 0:T * P].rearrange("p (t s) -> p t s", t=T)
                    g.affine_select(out=v, in_=v, compare_op=ALU.is_ge, fill=0.0, base=0,
                                    pattern=[[0, T], [1, P]], channel_multiplier=-1).then_inc(p_masked, 1)
                elif k == "LO":
                    h = s[1]
                    pool.wait_ge(p_hi_ready, HEADS * b + h + 1)
                    since(pool, pv_done, HEADS * b + h - 3)
                    g.tensor_tensor(p_lo[:, h % 4, :], p32[:, h % 4, :], p_hi[:, h % 4, :], ALU.subtract).then_inc(p_lo_ready, 1)
                elif k == "WO":
                    pool.wait_ge(stats2_ready, 2 * b + 2)
                    g.tensor_tensor(rs2[:, 0, :], mv2[:, :, 1], eps[:, :], ALU.add).then_inc(rs2_step, 1)
                    pool.wait_ge(rs2_step, 2 * b + 1)
                    g.tensor_tensor(rs2[:, 1, :], rs2[:, 0, :], half_neg[:, :], ALU.pow).then_inc(rs2_step, 1)
                elif k == "XE":
                    e = s[1]
                    pool.wait_ge(xe_hi_ready, E * f + e + 1)
                    g.tensor_tensor(xe_lo[:, e % 2, :], xe[:, e % 2, :], xe_hi[:, e % 2, :].bitcast(F32), ALU.subtract).then_inc(xe_lo_ready, 1)
                elif k == "WB":
                    g.memset(b2_f, 0.0).then_inc(b2_f_cleared, 1)
                    g.memset(mean_w, 1.0 / D)
                    g.memset(pick_f, 0.0).then_inc(picks_set, 1)
                    pool.wait_ge(picks_set, 1)
                    g.affine_select(out=pick_f, in_=pick_f, compare_op=ALU.not_equal, fill=1.0, base=0,
                                    pattern=[[-1, E]], channel_multiplier=1).then_inc(picks_set, 1)
                    pool.wait_ge(picks_set, 2)
                    g.affine_select(out=pick_f, in_=pick_f, compare_op=ALU.not_equal, fill=1.0, base=-32,
                                    pattern=[[-1, E]], channel_multiplier=1).then_inc(picks_set, 1)
                elif k == "W":
                    n, e = s[1], s[1] % E
                    if n < E:
                        pool.wait_ge(w_hi_ready, n + 1)
                        g.tensor_tensor(w1_lo[:, e, :], w1c[:, n % 2, :], w1_hi[:, e, :].bitcast(F32), ALU.subtract).then_inc(w1_lo_ready, 1)
                    elif n == E:
                        pool.wait_ge(w1_mean, E)
                        pool.wait_ge(b2_hi_ready, 2)
                        g.memset(m_tok[:, :, :], 0.0).then_inc(m_tok_cleared, 1)

            all_passes(pool, "gpsimd", one)

        @block.scalar
        def _(act):
            a = nc.scalar
            copy = ACT.Copy

            def one(p, s, c, b, f, late):
                k = s[0]
                bank = ring_bank(p, s) if k in RING_STEPS else None
                if k == "YT":
                    ring_full(act, p, s, c)
                    if isinstance(b, int):
                        act.wait_ge(norm_loaded, 16 * 2)
                    since(act, x1_ready, b - 1)
                    a.activation(y_t[:, :], bank[:, :], ACT.Identity, bias=lnb[:, 0:1], scale=lnw[:, 0:1]).then_inc(y_t_ready, 1)
                elif k == "PJ":
                    i = s[1]
                    ring_full(act, p, s, c)
                    since(act, v3_ready, b)
                    a.activation(vr[:, i, :, :], bank[:, 2 * P:3 * P].rearrange("p (h e) -> p h e", e=HD), copy).then_inc(v_raw_ready, 1)
                    if isinstance(b, int) and b == 0:
                        act.wait_ge(qk_cleared, 1)
                    v = qk[:, i, :, :, 0:HD].rearrange("p k h e -> p (k h) e")
                    a.activation(v.bitcast(F32R), bank[:, 0:2 * P].rearrange("p (h e) -> p h e", e=HD),
                                 copy).then_inc(qk_hi_ready, 1)
                elif k == "VS":
                    act.wait_ge(v_raw_ready, T * b + T)
                    since(act, pv_done, HEADS * b)
                    a.activation(v_op[:, :, :, 0:HD], vr[:, :, :, :], copy).then_inc(v1_ready, 1)
                elif k == "KT":
                    g = s[1]
                    ring_full(act, p, s, c)
                    if isinstance(b, int):
                        act.wait_ge(kz_cleared, 1)
                    for hh in range(HG):
                        rows = slice(R * hh, R * hh + R)
                        a.activation(kz[rows, g % 2, hh, :], bank[rows, :], copy).then_inc(kz_ready, 1)
                elif k == "QT":
                    g = s[1]
                    ring_full(act, p, s, c)
                    a.activation(q1[:, g % 2, :], bank[:, :], copy).then_inc(q1_ready, 1)
                elif k == "QM":
                    g = s[1]
                    ring_full(act, p, s, c)
                    a.activation(q2[:, g % 2, :], bank[:, :], copy).then_inc(q2_ready, 1)
                elif k == "ST":
                    g, u = s[1], s[2]
                    pair, v, head = unit(g, u)
                    act.wait_ge(st_filled, 40 * b + 10 * g + u + 1)
                    since(act, p_lo_ready, HEADS * b + 4 * g + 2 * pair - 2)
                    slot = (4 * g + head) % 4
                    if v in (0, 2):
                        dst, src = p32[:, slot, 0:512], st_ps[:, (10 * g + u) % 2, :]
                    elif v in (1, 3):
                        dst, src = p32[:, slot, 512:1024], st_ps[:, (10 * g + u) % 2, :]
                    else:
                        dst = p32[:, 2 * pair:2 * pair + 2, 1024:1280]
                        src = st_ps[:, (10 * g + u) % 2, :].rearrange("p (h s) -> p h s", h=2)
                    a.activation(dst, src, ACT.Exp, scale=SCALE).then_inc(exp_ready, 1)
                elif k == "AT":
                    ring_full(act, p, s, c)
                    a.activation(a_t[:, :], bank[:, :], copy).then_inc(a_t_ready, 1)
                elif k == "X2T":
                    ring_full(act, p, s, c)
                    if isinstance(b, int):
                        act.wait_ge(w2_lo_ready, E)
                    since(act, xe_ready, E * b)
                    a.activation(x2_t[:, :], bank[:, :], copy).then_inc(x2_t_ready, 1)
                elif k == "X1K":
                    act.wait_ge(x1_ready, f + 1)
                    since(act, ob_ready, f)
                    a.activation(x1_keep[:, :, :], x1[:, :, :], copy).then_inc(x1_kept, 1)
                elif k == "GE":
                    act.wait_ge(gate_step, 8 * b + 3)
                    a.activation(gexp[:, :, :], gate[:, :, :], ACT.Exp).then_inc(gexp_ready, 1)
                elif k == "MKT":
                    ring_full(act, p, s, c)
                    since(act, xe_ready, E * b)
                    a.activation(m_t[:, :], bank[:, :], copy).then_inc(m_t_ready, 1)
                elif k == "XE":
                    e = s[1]
                    act.wait_ge(xe_ready, E * f + e + 1)
                    a.activation(xe_hi[:, e % 2, :], xe[:, e % 2, :], copy).then_inc(xe_hi_ready, 1)
                elif k == "L1":
                    n = s[1]
                    act.wait_ge(l1_filled, L1_USES * f + L1_AT[s] + 1)
                    since(act, l2_done, N1 * f + max(n - 2, 0))
                    a.activation(h_hi[:, n % 3, :], l1_ps[:, L1_AT[s] % 2, :], ACT.Relu).then_inc(h_hi_ready, 1)
                elif k == "WB":
                    act.wait_ge(picks_set, 3)
                    a.activation(pick[:, :], pick_f, copy).then_inc(pick_ready, 1)
                    act.wait_ge(consts_loaded, 16 * CONSTS)
                    a.activation(b1_s[:, :], b1_s[:, :], copy, scale=-1.0 / D).then_inc(b1_scaled, 1)
                    a.activation(b2_x[:, :], b2_f, copy).then_inc(b2_hi_ready, 1)
                elif k == "W":
                    n, e = s[1], s[1] % E
                    if n < E:
                        act.wait_ge(w1_centred, n + 1)
                        a.activation(w1_hi[:, e, :], w1c[:, n % 2, :], copy).then_inc(w_hi_ready, 1)
                    else:
                        act.wait_ge(stage_loaded[n % STAGES], 16 * (n // STAGES + 1))
                        a.activation(w2_hi[:, C * e:C * e + C, :], stage[n % STAGES].rearrange("p (c d) -> p c d", c=C),
                                     copy).then_inc(w_hi_ready, 1)
                elif k == "OA":
                    act.wait_ge(l2_done, N1 * f + N1)
                    since(act, ot_filled, f)
                    a.activation(acc_s[:, :], acc_ps[:, :], copy).then_inc(acc_saved, 1)

            all_passes(act, "scalar", one)

        @block.vector
        def _(dve):
            v = nc.vector

            def norm_stats(src, stats, mv, ready, z):
                for i in range(T):
                    last = v.bn_stats(stats[:, i, :], src[:, i, :])
                last.then_inc(ready, 1)
                dve.wait_ge(ready, z + 1)
                apart(dve)
                for i in range(T):
                    last = v.bn_aggr(mv[:, i, :], stats[:, i, :])
                last.then_inc(ready, 1)

            def one(p, s, c, b, f, late):
                k = s[0]
                bank = ring_bank(p, s) if k in RING_STEPS else None
                if k == "LN1":
                    dve.wait_ge(x_loaded, 16 * b + 16)
                    norm_stats(xb, stats, mv, stats_ready, 2 * b)
                    if isinstance(b, int) and b == 0:
                        v.memset(kz[:, :, :, :].bitcast(F32), 0.0).then_inc(kz_cleared, 1)
                        v.memset(v_op[:, :, :, 3 * HD:VW], 1.0)
                elif k == "YN":
                    dve.wait_ge(rstd_ready, b + 1)
                    since(dve, x2_t_ready, b - 1)
                    for i in range(T):
                        last = v.tensor_scalar(yn[:, i, :], xb[:, i, :], mv[:, i, 0:1], rs[:, 0, i:i + 1], ALU.subtract, ALU.mult)
                    last.then_inc(yn_ready, 1)
                elif k == "XN":
                    dve.wait_ge(rs_step, 6 * b + 6)
                    since(dve, x1_ready, b)
                    for i in range(T):
                        last = v.tensor_scalar(xn[:, i, :], xb[:, i, :], mv[:, i, 0:1], rs[:, 1, i:i + 1], ALU.subtract, ALU.mult)
                    last.then_inc(xn_ready, 1)
                elif k == "PJ":
                    i = s[1]
                    dve.wait_ge(qk_hi_ready, T * b + i + 1)
                    v.tensor_copy(qk[:, i, 1, :, HD:2 * HD], qk[:, i, 1, :, 0:HD])
                    v.tensor_copy(qk[:, i, 0, :, 2 * HD:3 * HD], qk[:, i, 0, :, 0:HD])
                    v.tensor_tensor(qk[:, i, 0, :, HD:2 * HD], bank[:, 0:P].rearrange("p (h e) -> p h e", e=HD),
                                    qk[:, i, 0, :, 0:HD], ALU.subtract)
                    v.tensor_tensor(qk[:, i, 1, :, 2 * HD:3 * HD], bank[:, P:2 * P].rearrange("p (h e) -> p h e", e=HD),
                                    qk[:, i, 1, :, 0:HD], ALU.subtract).then_inc(qk_lo_ready, 1)
                elif k == "VS":
                    dve.wait_ge(v1_ready, b + 1)
                    v.tensor_tensor(vr[:, :, :, :], vr[:, :, :, :], v_op[:, :, :, 0:HD], ALU.subtract).then_inc(v_rest_ready, 1)
                    dve.wait_ge(v_rest_ready, b + 1)
                    v.tensor_copy(v_op[:, :, :, HD:2 * HD], vr[:, :, :, :]).then_inc(v2_ready, 1)
                elif k == "MX":
                    g, u = s[1], s[2]
                    pair, w, head = unit(g, u)
                    h = HG * g + head
                    ring_full(dve, p, s, c)
                    blocks = bank[:, :].rearrange("p (k s) -> p k s", k=4)
                    if w in (0, 2):
                        dst = bmax[:, h, 0:4]
                    elif w in (1, 3):
                        dst = bmax[:, h, 4:8]
                    else:
                        dst = bmax[:, HG * g + 2 * pair:HG * g + 2 * pair + 2, 8:10]
                        blocks = bank[:, :].rearrange("p (h k s) -> p h k s", h=2, k=2)
                    v.tensor_reduce(dst, blocks, X, ALU.max).then_inc(bmax_ready, 1)
                elif k == "NM":
                    g = s[1]
                    dve.wait_ge(bmax_ready, 40 * b + UNITS * g + UNITS)
                    dve.wait_ge(m_cleared, b + 1)
                    hs = slice(HG * g, HG * g + HG)
                    for i, (lo, hi) in enumerate(((7, 8), (8, 10), (4, 7), (0, 4))):
                        last = v.tensor_reduce(nmax[:, i, :], bmax[:, hs, lo:hi], X, ALU.max, negate=True)
                    last.then_inc(nmax_ready, 1)
                    dve.wait_ge(nmax_ready, HG * b + g + 1)
                    v.tensor_copy(qk[:, :, 0, hs, 3 * HD].bitcast(F32R), nmax[:, :, :]).then_inc(m_hi_ready, 1)
                    dve.wait_ge(m_hi_ready, HG * b + g + 1)
                    v.tensor_tensor(qk[:, :, 0, hs, 3 * HD + 1], nmax[:, :, :], qk[:, :, 0, hs, 3 * HD],
                                    ALU.subtract).then_inc(m_ready, 1)
                elif k == "PH":
                    h = s[1]
                    dve.wait_ge(p_masked, HEADS * b + h + 1)
                    since(dve, pv_done, HEADS * b + h - 3)
                    v.tensor_copy(p_hi[:, h % 4, :], p32[:, h % 4, :]).then_inc(p_hi_ready, 1)
                elif k == "ON":
                    g = s[1]
                    dve.wait_ge(pv_done, HEADS * b + HG * g + HG)
                    o = pv_ps[:, :].rearrange("p (n c) -> p n c", c=VW)
                    v.tensor_reduce(osum[:, :, :], o[:, :, 0:3 * HD].rearrange("p n (k e) -> p n e k", k=3), X, ALU.add)
                    v.reciprocal(rden[:, :], o[:, :, 3 * HD]).then_inc(pv_read, 1)
                    dve.wait_ge(pv_read, HG * b + g + 1)
                    for i in range(T):
                        r = rden[:, HG * i:HG * i + HG].rearrange("p (h a) -> p h a", a=1).broadcast_to([P, HG, HD])
                        last = v.tensor_tensor(attn[:, i, HG * g:HG * g + HG, :], osum[:, HG * i:HG * i + HG, :], r, ALU.mult)
                    last.then_inc(attn_ready, 1)
                    dve.wait_ge(attn_ready, HG * b + g + 1)
                elif k == "WO":
                    ring_full(dve, p, s, c)
                    if isinstance(b, int):
                        dve.wait_ge(w2_lo_ready, E)
                    dve.wait_ge(xr_ready, b + 1)
                    since(dve, x1_kept, b)
                    v.tensor_tensor(x1[:, :, :], bank[:, :].rearrange("p (t d) -> p t d", t=T), xr[:, :, :],
                                    ALU.add).then_inc(x1_ready, 1)
                    dve.wait_ge(x1_ready, b + 1)
                    norm_stats(x1, stats2, mv2, stats2_ready, 2 * b)
                elif k == "X2N":
                    dve.wait_ge(rs2_step, 2 * b + 2)
                    dve.wait_ge(y_t_ready, after_next(b))
                    for i in range(T):
                        last = v.tensor_scalar(xn2[:, i, :], x1[:, i, :], mv2[:, i, 0:1], rs2[:, 1, i:i + 1], ALU.subtract, ALU.mult)
                    last.then_inc(xn2_ready, 1)
                elif k == "GT":
                    z = 8 * b
                    ring_full(dve, p, s, c)
                    v.tensor_copy(gate[:, :, :], bank[:, 0:T * E].rearrange("p (t e) -> p t e", t=T)).then_inc(gate_step, 1)
                    dve.wait_ge(gate_step, z + 1)
                    apart(dve)
                    for i in range(T):
                        last = v.max(top[:, i, :], gate[:, i, :])
                    last.then_inc(gate_step, 1)
                    dve.wait_ge(gate_step, z + 2)
                    v.tensor_tensor(gsel[:, :, :], gate[:, :, :], top[:, :, 1:2].broadcast_to([P, T, E]), ALU.is_ge)
                    v.tensor_tensor(gate[:, :, :], gate[:, :, :], top[:, :, 0:1].broadcast_to([P, T, E]), ALU.subtract).then_inc(gate_step, 1)
                elif k == "GE":
                    z = 8 * b
                    dve.wait_ge(gexp_ready, b + 1)
                    v.tensor_tensor(gsel[:, :, :], gexp[:, :, :], gsel[:, :, :], ALU.mult).then_inc(gate_step, 1)
                    dve.wait_ge(gate_step, z + 4)
                    v.tensor_reduce(gsum[:, :], gsel[:, :, :], X, ALU.add).then_inc(gate_step, 1)
                    dve.wait_ge(gate_step, z + 5)
                    v.reciprocal(gsum[:, :], gsum[:, :]).then_inc(gate_step, 1)
                    dve.wait_ge(gate_step, z + 6)
                    v.tensor_tensor(gate[:, :, :], gsel[:, :, :], gsum[:, :].rearrange("p (t a) -> p t a", a=1).broadcast_to([P, T, E]),
                                    ALU.mult).then_inc(gate_step, 1)
                    dve.wait_ge(gate_step, z + 7)
                    if isinstance(b, int):
                        dve.wait_ge(m_tok_cleared, 1)
                    v.tensor_scalar(m_tok[:, :, 0:E].bitcast(F32R), gate[:, :, :], 1.0 / E, None, ALU.mult)
                    v.tensor_scalar(m_tok[:, :, 64:64 + E].bitcast(F32R), gate[:, :, :], 1.0 / E, None, ALU.mult).then_inc(gate_step, 1)
                    dve.wait_ge(gate_step, z + 8)
                    v.scalar_tensor_tensor(out=m_tok[:, :, 32:32 + E], in0=gate[:, :, :], scalar=1.0 / E, in1=m_tok[:, :, 0:E],
                                           op0=ALU.mult, op1=ALU.subtract).then_inc(m_tok_ready, 1)
                elif k == "XE":
                    e = s[1]
                    dve.wait_ge(l1_filled, L1_USES * f + L1_AT[s] + 1)
                    dve.wait_ge(x2_t_ready, f + 1)
                    since(dve, xe_lo_ready, E * f + max(e - 1, 0))
                    v.scalar_tensor_tensor(out=xe[:, e % 2, :], in0=x2_t[:, :], scalar=1.0, in1=l1_ps[:, L1_AT[s] % 2, :],
                                           op0=ALU.add, op1=ALU.mult).then_inc(xe_ready, 1)
                elif k == "WB":
                    dve.wait_ge(b2_hi_ready, 1)
                    v.tensor_tensor(b2_x[64:64 + R, :], b2_f[64:64 + R, :], b2_x[64:64 + R, :].bitcast(F32), ALU.subtract).then_inc(b2_hi_ready, 1)
                elif k == "W" and s[1] >= E:
                    n, e = s[1], s[1] - E
                    dve.wait_ge(w_hi_ready, n + 1)
                    v.tensor_tensor(w2_lo[:, C * e:C * e + C, :], stage[n % STAGES].rearrange("p (c d) -> p c d", c=C),
                                    w2_hi[:, C * e:C * e + C, :].bitcast(F32), ALU.subtract).then_inc(w2_lo_ready, 1)
                elif k == "W":
                    e = s[1]
                    dve.wait_ge(w1_mean, e + 1)
                    if e >= 2:
                        dve.wait_ge(w1_lo_ready, e - 1)
                    v.tensor_tensor(w1c[:, e % 2, :], stage[e % STAGES], l1_ps[:, e % 2, :], ALU.subtract).then_inc(w1_centred, 1)
                elif k == "L1":
                    n = s[1]
                    dve.wait_ge(h_hi_ready, N1 * f + n + 1)
                    since(dve, l2_done, N1 * f + max(n - 2, 0))
                    v.scalar_tensor_tensor(out=h_lo[:, n % 3, :], in0=l1_ps[:, L1_AT[s] % 2, :], scalar=0.0,
                                           in1=h_hi[:, n % 3, :].bitcast(F32), op0=ALU.max, op1=ALU.subtract).then_inc(h_lo_ready, 1)
                elif k == "OT":
                    dve.wait_ge(ot_filled, f + 1)
                    since(dve, out_stored, 16 * f)
                    dve.wait_ge(x1_kept, f + 1)
                    v.tensor_tensor(ob[:, :, :], pv_ps[:, :].rearrange("p (t d) -> p t d", t=T), x1_keep[:, :, :],
                                    ALU.add).then_inc(ob_ready, 1)

            all_passes(dve, "vector", one)

        @block.tensor
        def _(pe):
            t = nc.tensor

            def turn(bank, src):
                for i in range(T):
                    last = t.transpose(bank[:, i * P:(i + 1) * P], src(i), ident[:, :])
                return last

            def one(p, s, c, b, f, late):
                k = s[0]
                if k in RING_STEPS:
                    ring_free(pe, p, s, c)
                    bank = ring_bank(p, s)
                elif s in L1_AT:
                    l1_free(pe, s, f)
                    bank = l1_ps[:, L1_AT[s] % 2, :]
                if k == "YT":
                    if isinstance(b, int):
                        pe.wait_ge(consts_built, 1)
                    pe.wait_ge(yn_ready, b + 1)
                    turn(bank, lambda i: yn[:, i, :]).then_inc(ring_filled, 1)
                elif k == "PJ":
                    i = s[1]
                    pe.wait_ge(y_t_ready, b + 1)
                    if isinstance(b, int) and b == 0:
                        pe.wait_ge(wqkv_loaded, 16)
                    t.matmul(bank[:, 0:3 * P], y_t[:, i * P:(i + 1) * P], wqkv_s[:, :], start=True, stop=True).then_inc(ring_filled, 1)
                elif k in ("KT", "QT"):
                    g = s[1]
                    pe.wait_ge(qk_lo_ready, T * b + T)
                    if k == "QT":
                        pe.wait_ge(m_cleared, b + 1)
                    which = 1 if k == "KT" else 0
                    turn(bank, lambda i: qk[:, i, which, HG * g:HG * g + HG, :].rearrange("p h r -> p (h r)")).then_inc(ring_filled, 1)
                elif k == "QM":
                    g = s[1]
                    pe.wait_ge(m_ready, HG * b + g + 1)
                    turn(bank, lambda i: qk[:, i, 0, HG * g:HG * g + HG, :].rearrange("p h r -> p (h r)")).then_inc(ring_filled, 1)
                elif k == "MX":
                    g, u = s[1], s[2]
                    pair, v, head = unit(g, u)
                    if u == 0:
                        pe.wait_ge(kz_ready, HEADS * b + HG * g + HG)
                        pe.wait_ge(q1_ready, HG * b + g + 1)

                    def rows(i, head, at):
                        n = (i + 1) * P
                        t.matmul(bank[:, at:at + n], q1[:, g % 2, i * P:(i + 1) * P], kz[:, g % 2, head, 0:n], start=True, stop=False)
                        return t.matmul(bank[:, at + n - P:at + n], ident_b[:, :], causal[:, :], start=False, stop=True)

                    if v in (0, 2):
                        last = rows(3, head, 0)
                    elif v in (1, 3):
                        rows(2, head, 0)
                        last = rows(0, head, 3 * P)
                    else:
                        rows(1, 2 * pair, 0)
                        last = rows(1, 2 * pair + 1, 2 * P)
                    last.then_inc(ring_filled, 1)
                elif k == "ST":
                    g, u = s[1], s[2]
                    pair, v, head = unit(g, u)
                    n = 10 * g + u
                    since(pe, exp_ready, 40 * b + n - 1)
                    if u == 0:
                        pe.wait_ge(q2_ready, HG * b + g + 1)
                    st = st_ps[:, n % 2, :]

                    def cols(j, head, lo, hi, at):
                        return t.matmul(st[:, at:at + (hi - lo) * P], kz[:, g % 2, head, j * P:(j + 1) * P],
                                        q2[:, g % 2, lo * P:hi * P], start=True, stop=True)

                    if v in (0, 2):
                        for j in range(T):
                            last = cols(j, head, j, j + 1, j * P)
                    elif v in (1, 3):
                        cols(0, head, 1, 4, 0)
                        last = cols(2, head, 3, 4, 3 * P)
                    else:
                        cols(1, 2 * pair, 2, 4, 0)
                        last = cols(1, 2 * pair + 1, 2, 4, 2 * P)
                    last.then_inc(st_filled, 1)
                elif k == "PV":
                    h = s[1]
                    pe.wait_ge(p_lo_ready, HEADS * b + h + 1)
                    if h == 0:
                        pe.wait_ge(v3_ready, b + 1)
                        since(pe, ob_ready, b - 1)
                    if h % HG == 0:
                        since(pe, pv_read, HG * b + h // HG)
                    at = {(j, j): j for j in range(T)}
                    at.update({(0, 1): 4, (0, 2): 5, (0, 3): 6, (2, 3): 7, (1, 2): 8, (1, 3): 9})
                    for i in range(T):
                        o = pv_ps[:, (HG * i + h % HG) * VW:(HG * i + h % HG) * VW + 3 * HD + 1]
                        for j in range(i + 1):
                            col = at[(j, i)] * P
                            rhs = v_op[:, j, h, 0:3 * HD + 1]
                            t.matmul(o, p_hi[:, h % 4, col:col + P], rhs, start=(j == 0), stop=False)
                            last = t.matmul(o, p_lo[:, h % 4, col:col + P], rhs, start=False, stop=(j == i))
                    last.then_inc(pv_done, 1)
                elif k == "AT":
                    pe.wait_ge(attn_ready, HG * b + HG)
                    turn(bank, lambda i: attn[:, i, :, :].rearrange("p h e -> p (h e)")).then_inc(ring_filled, 1)
                elif k == "WO":
                    pe.wait_ge(a_t_ready, b + 1)
                    if isinstance(b, int) and b == 0:
                        pe.wait_ge(consts_loaded, 16 * CONSTS)
                    for i in range(T):
                        last = t.matmul(bank[:, i * P:(i + 1) * P], a_t[:, i * P:(i + 1) * P], wo_s[:, :], start=True, stop=True)
                    last.then_inc(ring_filled, 1)
                elif k == "X2T":
                    pe.wait_ge(xn2_ready, b + 1)
                    turn(bank, lambda i: xn2[:, i, :]).then_inc(ring_filled, 1)
                elif k == "GT":
                    pe.wait_ge(x2_t_ready, b + 1)
                    for i in range(T):
                        last = t.matmul(bank[:, i * E:(i + 1) * E], x2_t[:, i * P:(i + 1) * P], wg_s[:, :], start=True, stop=True)
                    last.then_inc(ring_filled, 1)
                elif k == "MKT":
                    pe.wait_ge(m_tok_ready, b + 1)
                    turn(bank, lambda i: m_tok[:, i, :]).then_inc(ring_filled, 1)
                elif k == "W" and s[1] < E:
                    e = s[1]
                    pe.wait_ge(stage_loaded[e % STAGES], 16 * (e // STAGES + 1))
                    pe.wait_ge(b1_scaled, 1)
                    if e >= 2:
                        pe.wait_ge(w1_centred, e - 1)
                    t.matmul(l1_ps[:, e % 2, :], mean_w, stage[e % STAGES], start=True, stop=False)
                    t.matmul(l1_ps[:, e % 2, :], pick[0:E, e:e + 1].bitcast(F32).broadcast_to([E, P]), b1_s[:, :], start=False, stop=True).then_inc(w1_mean, 1)
                elif k == "XE":
                    e = s[1]
                    if e == 0:
                        pe.wait_ge(m_t_ready, f + 1)
                    if isinstance(f, int) and e == 0:
                        pe.wait_ge(w1_lo_ready, E)
                        pe.wait_ge(w2_lo_ready, E)
                    t.matmul(bank[:, :], pick[:, e:e + 1].broadcast_to([P, P]), m_t[:, :], start=True, stop=True).then_inc(l1_filled, 1)
                elif k == "ACC0":
                    since(pe, acc_saved, f)
                    pe.wait_ge(m_t_ready, f + 1)
                    pe.wait_ge(b2_hi_ready, 2)
                    t.matmul(acc_ps[:, :], b2_x[:, :], m_t[:, :], start=True, stop=False)
                elif k == "L1":
                    n = s[1]
                    e, chunk = n // C, n % C
                    if chunk == 0:
                        pe.wait_ge(xe_lo_ready, E * f + e + 1)
                    w = slice(chunk * P, chunk * P + P)
                    t.matmul(bank, w1_lo[:, e, w], xe_hi[:, e % 2, :], start=True, stop=False)
                    t.matmul(bank, w1_hi[:, e, w], xe_lo[:, e % 2, :], start=False, stop=False)
                    t.matmul(bank, w1_hi[:, e, w], xe_hi[:, e % 2, :], start=False, stop=True).then_inc(l1_filled, 1)
                elif k == "L2":
                    n = s[1]
                    pe.wait_ge(h_lo_ready, N1 * f + n + 1)
                    t.matmul(acc_ps[:, :], w2_lo[:, n, :], h_hi[:, n % 3, :], start=False, stop=False)
                    t.matmul(acc_ps[:, :], w2_hi[:, n, :], h_lo[:, n % 3, :], start=False, stop=False)
                    t.matmul(acc_ps[:, :], w2_hi[:, n, :], h_hi[:, n % 3, :], start=False, stop=(n == N1 - 1)).then_inc(l2_done, 1)
                elif k == "OT":
                    pe.wait_ge(acc_saved, f + 1)
                    groups = c if late else c + 1
                    pe.wait_ge(pv_read, HG * (min(groups, B) if isinstance(groups, int) else groups))
                    since(pe, ob_ready, f)
                    turn(pv_ps, lambda i: acc_s[:, i * P:(i + 1) * P]).then_inc(ot_filled, 1)

            all_passes(pe, "tensor", one)


_INS = ["x", "ln_w", "ln_b", "wqkv", "wo", "w_gate", "w1", "b1", "w2", "b2"]


def kernel(L0_attn_x, L0_attn_ln_w, L0_attn_ln_b, L0_attn_wq, L0_attn_wk, L0_attn_wv, L0_attn_wo,
           L0_ffn_W_gate, L0_ffn_W1, L0_ffn_b1, L0_ffn_W2, L0_ffn_b2):
    import numpy as _np
    import concourse.bacc as _bacc
    from concourse import mybir as _mybir
    from concourse.bass_utils import run_bass_kernel_spmd as _run

    def by_input(w):
        return _np.transpose(_np.asarray(w), (1, 0, 2)).reshape(w.shape[1], -1)

    wqkv = _np.concatenate([by_input(w) for w in (L0_attn_wq, L0_attn_wk, L0_attn_wv)], axis=1)
    given = [L0_attn_x, L0_attn_ln_w, L0_attn_ln_b, wqkv, L0_attn_wo, L0_ffn_W_gate, L0_ffn_W1, L0_ffn_b1, L0_ffn_W2, L0_ffn_b2]
    nc = _bacc.Bacc("TRN2", target_bir_lowering=False, num_devices=1)
    arrays, args = {}, []
    for name, a in zip(_INS, given):
        a = _np.ascontiguousarray(a)
        arrays[f"in_{name}_dram"] = a
        args.append(nc.dram_tensor(f"in_{name}_dram", a.shape, _mybir.dt.from_np(a.dtype), kind="ExternalInput").ap())
    out = nc.dram_tensor("out_dram", arrays["in_x_dram"].shape, _mybir.dt.float32, kind="ExternalOutput").ap()
    moe_block_kernel(nc, *args, out)
    r = _run(nc, [arrays], core_ids=[0])
    return r.results[0]["out_dram"]
```
